# Optimizing a Trainium2 kernel written in Bass

```python
import numpy as np
import jax
import jax.numpy as jnp

def _softmax(x, axis=-1):
    return jax.nn.softmax(x, axis=axis)

def _gelu(x):
    return jax.nn.gelu(x, approximate=True)

def _silu(x):
    return jax.nn.silu(x)

def _sigmoid(x):
    return jax.nn.sigmoid(x)

def _layernorm(x, axis=-1, eps=1e-05):
    m = jnp.mean(x, axis=axis, keepdims=True)
    v = jnp.var(x, axis=axis, keepdims=True)
    return (x - m) / jnp.sqrt(v + eps)

def _scatter_add(tgt, idx, src, axis=0):
    return tgt.at[idx].add(src)

def _segment_sum(src, seg, n):
    return jax.ops.segment_sum(src, seg, n)
kernel_name = 'mk_seq_preln_d1_jaxref_r8_66da82'

def setup_inputs(seed: int=0):
    np.random.seed(seed)
    _w = jnp.asarray

    def _L0_attn_setup():
        import jax, jax.numpy as jnp
        import numpy as np
        key = jax.random.key(seed)
        ks = jax.random.split(key, 6)
        Bsz, S, H, N = (4, 512, 128, 32)
        return {'x': jax.random.normal(ks[0], (Bsz, S, H), jnp.float32), 'A': jax.random.normal(ks[1], (N, N), jnp.float32) * 0.01, 'Bm': jax.random.normal(ks[2], (N, N), jnp.float32) * 0.01, 'C': jax.random.normal(ks[3], (H, N), jnp.float32) * 0.01, 'D': jnp.full((H,), 0.01, jnp.float32), 'W_in': jax.random.normal(ks[4], (N, H), jnp.float32) / np.sqrt(H).astype(np.float32), 'b_in': jnp.zeros((N,), jnp.float32)}
    _L0_attn_in = _L0_attn_setup()

    def _L0_ffn_setup():
        import jax, jax.numpy as jnp
        import numpy as np
        D_MODEL = 128
        NUM_EXPERTS = 8
        HIDDEN = 512
        TOP_K = 2
        key = jax.random.key(seed)
        ks = jax.random.split(key, 6)
        x = jax.random.normal(ks[0], (2, 128, D_MODEL), dtype=jnp.float32)
        gate_w = jax.random.normal(ks[1], (NUM_EXPERTS, D_MODEL), dtype=jnp.float32) * (1.0 / np.sqrt(D_MODEL))
        w1 = jax.random.normal(ks[2], (NUM_EXPERTS, HIDDEN, D_MODEL), dtype=jnp.float32) * (1.0 / np.sqrt(D_MODEL))
        b1 = jax.random.normal(ks[3], (NUM_EXPERTS, HIDDEN), dtype=jnp.float32) * 0.01
        w2 = jax.random.normal(ks[4], (NUM_EXPERTS, D_MODEL, HIDDEN), dtype=jnp.float32) * (1.0 / np.sqrt(HIDDEN))
        b2 = jax.random.normal(ks[5], (NUM_EXPERTS, D_MODEL), dtype=jnp.float32) * 0.01
        return {'x': x, 'gate_w': gate_w, 'w1': w1, 'b1': b1, 'w2': w2, 'b2': b2}
    _L0_ffn_in = _L0_ffn_setup()
    _d = {'L0_attn_x': _L0_attn_in['x'], 'L0_attn_A': _L0_attn_in['A'], 'L0_attn_Bm': _L0_attn_in['Bm'], 'L0_attn_C': _L0_attn_in['C'], 'L0_attn_D': _L0_attn_in['D'], 'L0_attn_W_in': _L0_attn_in['W_in'], 'L0_attn_b_in': _L0_attn_in['b_in'], 'L0_ffn_gate_w': _L0_ffn_in['gate_w'], 'L0_ffn_w1': _L0_ffn_in['w1'], 'L0_ffn_b1': _L0_ffn_in['b1'], 'L0_ffn_w2': _L0_ffn_in['w2'], 'L0_ffn_b2': _L0_ffn_in['b2']}
    _x0 = _d['L0_attn_x']
    _d['L0_attn_x'] = jax.random.normal(jax.random.fold_in(jax.random.key(seed), 1), (16, 256, 128), dtype=_x0.dtype)
    del _x0
    return _d

def reference(L0_attn_x, L0_attn_A, L0_attn_Bm, L0_attn_C, L0_attn_D, L0_attn_W_in, L0_attn_b_in, L0_ffn_gate_w, L0_ffn_w1, L0_ffn_b1, L0_ffn_w2, L0_ffn_b2):

    def _L0_attn_ref(x, A, Bm, C, D, W_in, b_in):
        import jax, jax.numpy as jnp
        import numpy as np
        u = jnp.einsum('bsh,nh->bsn', x, W_in) + b_in
        uB = jnp.einsum('bsn,mn->bsm', u, Bm)

        def step(h, uB_t):
            h = h @ A + uB_t
            return (h, h)
        h0 = jnp.zeros((x.shape[0], A.shape[0]), x.dtype)
        _, hs = jax.lax.scan(step, h0, jnp.swapaxes(uB, 0, 1))
        hs = jnp.swapaxes(hs, 0, 1)
        return jnp.einsum('bsn,hn->bsh', hs, C) + D

    def _L0_ffn_ref(x, gate_w, w1, b1, w2, b2):
        import jax, jax.numpy as jnp
        import numpy as np
        D_MODEL = 128
        NUM_EXPERTS = 8
        HIDDEN = 512
        TOP_K = 2
        B, S, D = x.shape
        xf = x.reshape(-1, D)
        T = xf.shape[0]
        gate_logits = xf @ gate_w.T
        gate_probs = jax.nn.softmax(gate_logits, axis=-1)
        topk_scores, topk_idx = jax.lax.top_k(gate_probs, TOP_K)
        topk_scores = topk_scores / jnp.sum(topk_scores, axis=-1, keepdims=True)
        combine = jnp.zeros((T, NUM_EXPERTS), dtype=x.dtype)
        combine = combine.at[jnp.arange(T)[:, None], topk_idx].set(topk_scores)
        h = jax.nn.relu(jnp.einsum('td,ehd->teh', xf, w1) + b1)
        expert_out = jnp.einsum('teh,edh->ted', h, w2) + b2
        out = jnp.einsum('ted,te->td', expert_out, combine)
        return out.reshape(B, S, D)
    x = L0_attn_x
    x = x + _L0_attn_ref(_layernorm(x, axis=-1), L0_attn_A, L0_attn_Bm, L0_attn_C, L0_attn_D, L0_attn_W_in, L0_attn_b_in)
    x = x + _L0_ffn_ref(_layernorm(x, axis=-1), L0_ffn_gate_w, L0_ffn_w1, L0_ffn_b1, L0_ffn_w2, L0_ffn_b2)
    return x

_drawn_inputs = setup_inputs


def setup_inputs(seed=0):
    import zlib

    import numpy as np

    out = dict(_drawn_inputs(seed))
    spreads = {'L0_attn_D': (0.009999999776482582, 0.6), 'L0_attn_b_in': (0.0, 0.8)}
    factors = {'L0_attn_A': 8.0,
     'L0_attn_Bm': 3.528,
     'L0_attn_C': 3.329,
     'L0_attn_W_in': 3.179,
     'L0_ffn_b1': 8.0,
     'L0_ffn_b2': 8.0}
    for name, (base, spread) in spreads.items():
        noise = np.random.default_rng([zlib.crc32(name.encode()), seed]).standard_normal(out[name].shape)
        drawn = base * np.exp(spread * noise) if base else spread * noise
        out[name] = jnp.asarray(drawn.astype(out[name].dtype))
    for name, factor in factors.items():
        out[name] = (out[name] * factor).astype(out[name].dtype)
    return out
```

```python
import concourse.bass as bass
from concourse import mybir
from contextlib import ExitStack

FP32 = mybir.dt.float32
ALU = mybir.AluOpType
ACT = mybir.ActivationFunctionType
AX = mybir.AxisListType

P = 128
D = 128
N = 32
J = 4
TILES = 8
COLS = TILES * J
SEQ_CHUNKS = 64
SEQS = 2
G = 4
GT = TILES // G
DOUBLINGS = 6
E = 8
HID = 512
HC = HID // P
EPS = 1e-5


def build(nc, x, A, AT, BmT, Bm, CT, Dv, W_in, b_in, gateT, w1T, b1, w2T, b2, out):
    ctx = ExitStack()
    with ctx:
        def sb(name, shape, dt=FP32):
            return ctx.enter_context(nc.sbuf_tensor(name, shape, dt))

        def sem(name):
            return ctx.enter_context(nc.semaphore(name))

        bank = [ctx.enter_context(nc.psum_tensor(f"bank{k}", [P, 512], FP32)) for k in range(8)]

        x_sb = sb("x_sb", [P, TILES, J, D])
        A_sb = sb("A_sb", [N, N])
        AT_sb = sb("AT_sb", [N, N])
        BmT_sb = sb("BmT_sb", [N, N])
        Bm_sb = sb("Bm_sb", [N, N])
        CT_sb = sb("CT_sb", [N, D])
        Win_sb = sb("Win_sb", [N, D])
        bin_sb = sb("bin_sb", [N, 1])
        Dbc = sb("Dbc", [P, D])
        gateT_sb = sb("gateT_sb", [D, E])
        w1_sb = sb("w1_sb", [D, E, HID])
        b1_sb = sb("b1_sb", [P, E * HC])
        w2_sb = sb("w2_sb", [P, E, HC, D])
        b2_sb = sb("b2_sb", [D, E])
        ident = sb("ident", [P, P])
        esel = sb("esel", [E, E, P])
        eiota = sb("eiota", [P, COLS, E])
        Apow = sb("Apow", [N, J + 1, N])
        ATpow = sb("ATpow", [N, J + 1, N])
        ATrep = sb("ATrep", [N, J + 1, G, N])
        sq = sb("sq", [N, DOUBLINGS, 2, N])
        sqrep = sb("sqrep", [N, DOUBLINGS, G, N])
        bd = sb("bd", [P, DOUBLINGS, P])
        Gst = sb("Gst", [D, (2 * J - 1) * N])
        Msum = sb("Msum", [N, J, N])
        v0 = sb("v0", [N, 1])
        BA = sb("BA", [N, P])
        hbias = sb("hbias", [P, 1])
        bdC = sb("bdC", [P, J, D])
        Rc = sb("Rc", [P, J, D])
        stats = sb("stats", [P, COLS, 6])
        mean = sb("mean", [P, COLS])
        var = sb("var", [P, COLS])
        sd = sb("sd", [P, COLS])
        rs = sb("rs", [P, COLS])
        tn = sb("tn", [P, COLS])
        xh = sb("xh", [P, TILES, J, D])
        xhT = sb("xhT", [D, TILES, J, P])
        hloc = sb("hloc", [P, TILES, P])
        ebuf = sb("ebuf", [P, GT * SEQS, SEQ_CHUNKS + 1])
        cbuf = sb("cbuf", [P, GT, P])
        lg = sb("lg", [P, COLS, E])
        comb = sb("comb", [P, COLS, E])
        tmp = sb("tmp", [P, 4, COLS, E])
        r1 = sb("r1", [P, 6, COLS])
        combT = sb("combT", [E, TILES, J * P])
        hsb = sb("hsb", [P, HC, 512])
        bcs = sb("bcs", [P, 512])
        tt = sb("tt", [P, 512])
        acc = sb("acc", [P, 512])

        s_small = sem("s_small")
        s_x = [sem(f"s_x{i}") for i in range(2)]
        s_w1 = sem("s_w1")
        s_w2 = sem("s_w2")
        s_id = sem("s_id")
        s_pool = sem("s_pool")
        s_pe = sem("s_pe")
        s_v = sem("s_v")
        s_a = sem("s_a")
        s_set = sem("s_set")
        s_st = sem("s_st")
        s_var = sem("s_var")
        s_sd = sem("s_sd")
        s_xh = sem("s_xh")
        s_T = sem("s_T")
        s_xhT = sem("s_xhT")
        s_H = sem("s_H")
        s_hloc = sem("s_hloc")
        s_e = sem("s_e")
        s_sc = sem("s_sc")
        s_car = sem("s_car")
        s_y = sem("s_y")
        s_x2 = sem("s_x2")
        s_xd = sem("s_xd")
        s_T2 = sem("s_T2")
        s_xhT2 = sem("s_xhT2")
        s_g = sem("s_g")
        s_exp = sem("s_exp")
        s_lgm = sem("s_lgm")
        s_cT = sem("s_cT")
        s_cTs = sem("s_cTs")
        s_up = sem("s_up")
        s_h = sem("s_h")
        s_bc = sem("s_bc")
        s_bcs = sem("s_bcs")
        s_dn = sem("s_dn")
        s_free = sem("s_free")
        s_add = sem("s_add")
        s_oT = sem("s_oT")
        s_yo = sem("s_yo")
        s_out = sem("s_out")

        block = ctx.enter_context(nc.Block())
        x_v = x.rearrange("(i q j) d -> i q (j d)", q=P, j=J)
        out_v = out.rearrange("(i q j) d -> i q (j d)", q=P, j=J)
        SMALL = 11 + G

        @block.sync
        def _(sp):
            for h in range(2):
                sp.dma_start(x_sb[:, 4 * h:4 * h + 4, :, :].rearrange("q i j d -> q i (j d)"),
                             x_v[4 * h:4 * h + 4].rearrange("i q n -> q i n")).then_inc(s_x[h], 16)
            sp.dma_start(w1_sb[:, :, :], w1T).then_inc(s_w1, 16)
            sp.dma_start(w2_sb[:, :, :, :], w2T).then_inc(s_w2, 16)
            with sp.Fori(0, TILES) as i:
                sp.wait_ge(s_yo, i + 1)
                sp.dma_start(out_v[bass.ds(i, 1)].rearrange("a q n -> q (a n)"),
                             x_sb[:, bass.ds(i, 1), :, :].rearrange("q a j d -> q (a j d)")).then_inc(s_out, 16)
            sp.wait_ge(s_out, 16 * TILES)

        @block.gpsimd
        def _(pool):
            nc.gpsimd.memset(ident[:], 0.0).then_inc(s_id, 1)
            nc.gpsimd.memset(esel[:], 1.0).then_inc(s_id, 1)
            nc.gpsimd.memset(bdC[:], 0.0).then_inc(s_id, 1)
            pool.wait_ge(s_id, 3)
            nc.gpsimd.affine_select(out=ident[:], in_=ident[:], compare_op=ALU.not_equal, fill=1.0, base=0,
                                    pattern=[[-1, P]], channel_multiplier=1).then_inc(s_pool, 1)
            nc.gpsimd.affine_select(out=esel[:], in_=esel[:], compare_op=ALU.is_equal, fill=0.0, base=0,
                                    pattern=[[-1, E], [0, P]], channel_multiplier=1).then_inc(s_pool, 1)
            nc.gpsimd.iota(eiota[:], [[0, COLS], [-1, E]], base=E, channel_multiplier=0,
                           allow_small_or_imprecise_dtypes=True).then_inc(s_pool, 1)
            pool.wait_ge(s_small, 16 * SMALL)
            with pool.Fori(0, TILES) as i:
                for h in range(2):
                    pool.wait_ge(s_x[h], 16)
                pool.wait_ge(s_xh, i + 1)
                nc.gpsimd.tensor_tensor(x_sb[:, i, :, :], x_sb[:, i, :, :],
                                        Dbc[:, :].unsqueeze(1).to_broadcast([P, J, D]), ALU.add).then_inc(s_xd, 1)

        @block.scalar
        def _(act):
            for dst, src in ((A_sb, A), (AT_sb, AT), (BmT_sb, BmT), (Bm_sb, Bm), (CT_sb, CT), (Win_sb, W_in),
                             (bin_sb, b_in), (gateT_sb, gateT), (b1_sb, b1), (b2_sb, b2)):
                act.dma_start(dst[:, :], src).then_inc(s_small, 16)
            act.dma_start(Dbc[:, :], Dv.rearrange("(a d) -> a d", a=1).to_broadcast([P, D])).then_inc(s_small, 16)
            act.wait_ge(s_id, 3)
            for g in range(G):
                act.dma_start(bdC[N * g:N * g + N, g, :], CT).then_inc(s_small, 16)

            def root(layer):
                act.wait_ge(s_var, layer + 1)
                nc.scalar.activation(sd[:, :], var[:, :], ACT.Sqrt).then_inc(s_sd, 1)

            root(0)
            with act.Fori(0, TILES) as i:
                act.wait_ge(s_T, i + 1)
                nc.scalar.activation(xhT[:, i, :, :], bank[0][:, :], ACT.Identity).then_inc(s_xhT, 1)
                act.wait_ge(s_H, i + 1)
                nc.scalar.activation(hloc[:, i, :], bank[1][:, 0:P], ACT.Identity,
                                     bias=hbias[:, :]).then_inc(s_hloc, 1)
            root(1)
            with act.Fori(0, TILES) as i:
                act.wait_ge(s_T2, i + 1)
                nc.scalar.activation(xhT[:, i, :, :], bank[0][:, :], ACT.Identity).then_inc(s_xhT2, 1)
            act.wait_ge(s_lgm, 1)
            nc.scalar.activation(tmp[:, 1, :, :], tmp[:, 0, :, :], ACT.Exp).then_inc(s_exp, 1)
            with act.Fori(0, TILES) as i:
                act.wait_ge(s_cT, i + 1)
                nc.scalar.activation(combT[:, i, :], bank[0][0:E, :], ACT.Identity).then_inc(s_cTs, 1)
            with act.Fori(0, TILES) as i:
                for e in range(E):
                    act.wait_ge(s_bc, E * i + e + 1)
                    act.wait_ge(s_free, E * i + e + 1)
                    nc.scalar.activation(bcs[:, :], bank[4][:, :], ACT.Identity).then_inc(s_bcs, 1)
                    for c in range(HC):
                        act.wait_ge(s_up, HC * (E * i + e) + c + 1)
                        nc.scalar.activation(hsb[:, c, :], bank[c][:, :], ACT.Relu,
                                             bias=b1_sb[:, HC * e + c:HC * e + c + 1]).then_inc(s_h, 1)

        @block.vector
        def _(dve):
            chain = [0]

            def link(ins):
                chain[0] += 1
                ins.then_inc(s_v, 1)
                dve.wait_ge(s_v, chain[0])

            nc.vector.memset(Gst[:], 0.0)
            nc.vector.memset(bd[:], 0.0)
            link(nc.vector.memset(ebuf[:], 0.0))

            dve.wait_ge(s_small, 16 * SMALL)
            dve.wait_ge(s_pool, 3)
            nc.vector.tensor_copy(Apow[:, 0, :], ident[0:N, 0:N])
            nc.vector.tensor_copy(ATpow[:, 0, :], ident[0:N, 0:N])
            nc.vector.tensor_copy(Apow[:, 1, :], A_sb[:, :])
            nc.vector.tensor_copy(ATpow[:, 1, :], AT_sb[:, :]).then_inc(s_set, 1)
            S = bank[7]
            dve.wait_ge(s_pe, 1)
            nc.vector.tensor_copy(v0[:, :], bank[5][0:N, 0:1])
            for k in range(2, J + 1):
                dve.wait_ge(s_pe, k)
                nc.vector.tensor_copy(Apow[:, k, :], S[0:N, 0:N])
                nc.vector.tensor_copy(ATpow[:, k, :], S[0:N, N:2 * N]).then_inc(s_set, 1)
            link(nc.vector.tensor_copy(sq[:, 0, :, :].rearrange("n a m -> n (a m)"), S[0:N, 0:2 * N]))
            for k in range(J + 1):
                nc.vector.tensor_copy(ATrep[:, k, :, :], ATpow[:, k, :].unsqueeze(1).to_broadcast([N, G, N]))
            nc.vector.tensor_copy(Msum[:, 0, :], Apow[:, 0, :])
            link(nc.vector.tensor_tensor(Msum[:, 1, :], Apow[:, 0, :], Apow[:, 1, :], ALU.add))
            link(nc.vector.tensor_tensor(Msum[:, 2, :], Msum[:, 1, :], Apow[:, 2, :], ALU.add))
            nc.vector.tensor_tensor(Msum[:, 3, :], Msum[:, 2, :], Apow[:, 3, :], ALU.add).then_inc(s_set, 1)
            for k in range(DOUBLINGS):
                nc.vector.tensor_copy(sqrep[:, k, :, :],
                                      sq[:, k, 1, :].unsqueeze(1).to_broadcast([N, G, N])).then_inc(s_set, 1)
                dve.wait_ge(s_pe, J + 1 + k)
                if k < DOUBLINGS - 1:
                    nc.vector.tensor_copy(sq[:, k + 1, :, :].rearrange("n a m -> n (a m)"), S[0:N, 0:2 * N])
                for g in range(G):
                    last = nc.vector.tensor_copy(bd[N * g:N * g + N, k, N * g:N * g + N],
                                                 S[N * g:N * g + N, 2 * N:3 * N])
                if k < DOUBLINGS - 1:
                    link(last)
                else:
                    last.then_inc(s_set, 1)
            dve.wait_ge(s_pe, J + 1 + DOUBLINGS)
            nc.vector.tensor_copy(BA[:, :], S[0:N, 0:P]).then_inc(s_set, 1)
            dve.wait_ge(s_pe, J + 2 + DOUBLINGS)
            nc.vector.tensor_copy(Gst[:, (J - 1) * N:(2 * J - 1) * N], S[:, 0:J * N])
            nc.vector.tensor_copy(hbias[:, :], S[:, J * N:J * N + 1]).then_inc(s_set, 1)
            dve.wait_ge(s_pe, J + 3 + DOUBLINGS)
            nc.vector.tensor_copy(Rc[:, :, :].rearrange("n j d -> n (j d)"), bank[6][:, :]).then_inc(s_set, 1)

            def statistics(i, src):
                for j in range(J):
                    last = nc.vector.bn_stats(stats[:, bass.ds(J * i + j, 1), :].rearrange("p a s -> p (a s)"),
                                              src[:, i, j, :])
                last.then_inc(s_st, 1)

            def moments(layer):
                dve.wait_ge(s_st, TILES * (layer + 1))
                nc.vector.tensor_tensor(mean[:, :], stats[:, :, 1], stats[:, :, 4], ALU.add)
                nc.vector.tensor_tensor(tn[:, :], stats[:, :, 1], stats[:, :, 4], ALU.subtract)
                link(nc.vector.tensor_tensor(var[:, :], stats[:, :, 2], stats[:, :, 5], ALU.add))
                nc.vector.tensor_scalar(mean[:, :], mean[:, :], 0.5, None, ALU.mult)
                link(nc.vector.tensor_tensor(tn[:, :], tn[:, :], tn[:, :], ALU.mult))
                link(nc.vector.tensor_scalar(tn[:, :], tn[:, :], 0.25, EPS, ALU.mult, ALU.add))
                nc.vector.scalar_tensor_tensor(var[:, :], var[:, :], 1.0 / D, tn[:, :],
                                               ALU.mult, ALU.add).then_inc(s_var, 1)
                dve.wait_ge(s_sd, layer + 1)
                link(nc.vector.reciprocal(rs[:, :], sd[:, :]))
                link(nc.vector.tensor_tensor(tn[:, :], rs[:, :], rs[:, :], ALU.mult))
                link(nc.vector.tensor_tensor(tn[:, :], tn[:, :], var[:, :], ALU.mult))
                link(nc.vector.tensor_scalar(tn[:, :], tn[:, :], -0.5, 1.5, ALU.mult, ALU.add))
                link(nc.vector.tensor_tensor(rs[:, :], rs[:, :], tn[:, :], ALU.mult))

            def normalise(i, src):
                for j in range(J):
                    last = nc.vector.tensor_scalar(xh[:, i, j, :], src[:, i, j, :],
                                                   mean[:, bass.ds(J * i + j, 1)], rs[:, bass.ds(J * i + j, 1)],
                                                   ALU.subtract, ALU.mult)
                last.then_inc(s_xh, 1)

            for h in range(2):
                dve.wait_ge(s_x[h], 16)
            with dve.Fori(0, TILES) as i:
                statistics(i, x_sb)
            moments(0)
            with dve.Fori(0, TILES) as i:
                normalise(i, x_sb)

            dve.wait_ge(s_hloc, TILES)
            for g in range(G):
                last = nc.vector.tensor_copy(
                    ebuf[N * g:N * g + N, :, 1:],
                    hloc[P - N:P, GT * g:GT * g + GT, :].rearrange("n t (s c) -> n (t s) c", s=SEQS))
            last.then_inc(s_e, 1)
            for k in range(DOUBLINGS):
                step = 1 << k
                dve.wait_ge(s_sc, k + 1)
                dve.wait_ge(s_e, k + 1)
                nc.vector.tensor_tensor(
                    ebuf[:, :, 1 + step:], ebuf[:, :, 1 + step:],
                    bank[2][:, 0:GT * P].rearrange("n (s c) -> n s c", c=SEQ_CHUNKS)[:, :, 0:SEQ_CHUNKS - step],
                    ALU.add).then_inc(s_e, 1)
            dve.wait_ge(s_e, DOUBLINGS + 1)
            nc.vector.tensor_copy(cbuf[:, :, :].rearrange("n t (s c) -> n (t s) c", s=SEQS),
                                  ebuf[:, :, 0:SEQ_CHUNKS]).then_inc(s_car, 1)

            dve.wait_ge(s_xd, TILES)
            for i in range(TILES):
                dve.wait_ge(s_y, i + 1)
                x_tile = x_sb[:, i, :, :].rearrange("q j d -> q (j d)")
                nc.vector.tensor_tensor(x_tile, x_tile, bank[i % 2][:, :], ALU.add).then_inc(s_x2, 1)
                dve.wait_ge(s_x2, i + 1)
                statistics(i, x_sb)
            moments(1)
            with dve.Fori(0, TILES) as i:
                normalise(i, x_sb)

            dve.wait_ge(s_g, 1)
            l, ex, pr, oh = tmp[:, 0, :, :], tmp[:, 1, :, :], tmp[:, 2, :, :], tmp[:, 3, :, :]

            def wide(a):
                return a.unsqueeze(2).to_broadcast([P, COLS, E])

            G3 = bank[5][:, 0:COLS * E].rearrange("p (t e) -> p t e", e=E)
            link(nc.vector.tensor_copy(lg[:, :, :], G3))
            link(nc.vector.tensor_reduce(r1[:, 0, :], lg[:, :, :], AX.X, ALU.max))
            nc.vector.tensor_tensor(l, lg[:, :, :], wide(r1[:, 0, :]), ALU.subtract).then_inc(s_lgm, 1)
            dve.wait_ge(s_lgm, 1)
            link(nc.vector.scalar_tensor_tensor(pr, l, 0.0, eiota[:, :, :], ALU.is_equal, ALU.mult))
            link(nc.vector.tensor_reduce(r1[:, 1, :], pr, AX.X, ALU.max))
            link(nc.vector.tensor_tensor(oh, eiota[:, :, :], wide(r1[:, 1, :]), ALU.is_equal))
            link(nc.vector.scalar_tensor_tensor(pr, oh, -3e38, l, ALU.mult, ALU.add))
            link(nc.vector.tensor_reduce(r1[:, 2, :], pr, AX.X, ALU.max))
            link(nc.vector.tensor_tensor(pr, pr, wide(r1[:, 2, :]), ALU.is_equal))
            link(nc.vector.tensor_tensor(pr, pr, eiota[:, :, :], ALU.mult))
            link(nc.vector.tensor_reduce(r1[:, 3, :], pr, AX.X, ALU.max))
            link(nc.vector.tensor_tensor(pr, eiota[:, :, :], wide(r1[:, 3, :]), ALU.is_equal))
            link(nc.vector.tensor_tensor(oh, oh, pr, ALU.add))
            dve.wait_ge(s_exp, 1)
            link(nc.vector.tensor_reduce(r1[:, 4, :], ex, AX.X, ALU.add))
            link(nc.vector.reciprocal(r1[:, 4, :], r1[:, 4, :]))
            link(nc.vector.tensor_tensor(pr, ex, wide(r1[:, 4, :]), ALU.mult))
            link(nc.vector.tensor_tensor(pr, pr, oh, ALU.mult))
            link(nc.vector.tensor_reduce(r1[:, 4, :], pr, AX.X, ALU.add))
            link(nc.vector.reciprocal(r1[:, 4, :], r1[:, 4, :]))
            nc.vector.tensor_tensor(comb[:, :, :], pr, wide(r1[:, 4, :]), ALU.mult).then_inc(s_free, 1)

            with dve.Fori(0, TILES) as i:
                for e in range(E):
                    if e >= 2:
                        dve.wait_ge(s_add, (E - 1) * i + e - 1)
                    dve.wait_ge(s_bcs, E * i + e + 1)
                    dve.wait_ge(s_dn, E * i + e + 1)
                    nc.vector.scalar_tensor_tensor((tt if e else acc)[:, :], bank[5][:, :], b2_sb[:, e:e + 1],
                                                   bcs[:, :], ALU.add, ALU.mult).then_inc(s_free, 1)
                    if e:
                        dve.wait_ge(s_free, E * i + e + 2)
                        nc.vector.tensor_tensor(acc[:, :], acc[:, :], tt[:, :], ALU.add).then_inc(s_add, 1)
                dve.wait_ge(s_oT, i + 1)
                x_tile = x_sb[:, bass.ds(i, 1), :, :].rearrange("q a j d -> q (a j d)")
                nc.vector.tensor_tensor(x_tile, x_tile, bank[6][:, :], ALU.add).then_inc(s_yo, 1)

        @block.tensor
        def _(pe):
            S = bank[7]
            mm = nc.tensor.matmul
            pe.wait_ge(s_small, 16 * SMALL)
            pe.wait_ge(s_pool, 3)
            pe.wait_ge(s_set, 1)
            mm(bank[5][0:N, 0:1], BmT_sb[:, :], bin_sb[:, :], start=True, stop=True).then_inc(s_pe, 1)
            for k in range(2, J + 1):
                pe.wait_ge(s_set, k - 1)
                mm(S[0:N, 0:N], AT_sb[:, :], Apow[:, k - 1, :], start=True, stop=True)
                mm(S[0:N, N:2 * N], A_sb[:, :], ATpow[:, k - 1, :], start=True, stop=True).then_inc(s_pe, 1)
            for k in range(DOUBLINGS):
                pe.wait_ge(s_set, J + 2 + k)
                mm(S[0:N, 0:N], sq[:, k, 1, :], sq[:, k, 0, :], start=True, stop=True)
                mm(S[0:N, N:2 * N], sq[:, k, 0, :], sq[:, k, 1, :], start=True, stop=True)
                mm(S[:, 2 * N:3 * N], sqrep[:, k, :, :].rearrange("n g m -> n (g m)"), ident[0:N, 0:N],
                   start=True, stop=True).then_inc(s_pe, 1)
            base = J + 1 + DOUBLINGS
            pe.wait_ge(s_set, base + 1)
            mm(S[0:N, 0:P], Bm_sb[:, :], Apow[:, 0:J, :].rearrange("n j m -> n (j m)"),
               start=True, stop=True).then_inc(s_pe, 1)
            pe.wait_ge(s_set, base + 2)
            mm(S[:, 0:P], Win_sb[:, :], BA[:, :], start=True, stop=True)
            mm(S[:, P:P + 1], Msum[:, :, :].rearrange("n j m -> n (j m)"), v0[:, :],
               start=True, stop=True).then_inc(s_pe, 1)
            for j in range(J):
                last = mm(bank[6][:, j * D:j * D + D], ATrep[:, j + 1, :, :].rearrange("n g m -> n (g m)"),
                          CT_sb[:, :], start=True, stop=True)
            last.then_inc(s_pe, 1)
            pe.wait_ge(s_set, base + 4)

            for i in range(TILES):
                pe.wait_ge(s_xh, i + 1)
                for j in range(J):
                    last = nc.tensor.transpose(bank[0][:, j * P:j * P + P], xh[:, i, j, :], ident[:, :])
                last.then_inc(s_T, 1)
                pe.wait_ge(s_xhT, i + 1)
                for j in range(J):
                    last = mm(bank[1][:, 0:P], Gst[:, (J - 1 - j) * N:(2 * J - 1 - j) * N], xhT[:, i, j, :],
                              start=(j == 0), stop=(j == J - 1))
                last.then_inc(s_H, 1)

            for k in range(DOUBLINGS):
                pe.wait_ge(s_e, k + 1)
                mm(bank[2][:, 0:GT * P].rearrange("n (s c) -> n s c", c=SEQ_CHUNKS), bd[:, k, :], ebuf[:, :, 1:],
                   start=True, stop=True).then_inc(s_sc, 1)

            pe.wait_ge(s_car, 1)
            for i in range(TILES):
                g = i // GT
                if i >= 2:
                    pe.wait_ge(s_x2, i - 1)
                mm(bank[i % 2][:, :], hloc[:, i, :], bdC[:, :, :].rearrange("n j d -> n (j d)"),
                   start=True, stop=False)
                mm(bank[i % 2][:, :], cbuf[N * g:N * g + N, i % GT, :],
                   Rc[N * g:N * g + N, :, :].rearrange("n j d -> n (j d)"), start=False, stop=True).then_inc(s_y, 1)
            pe.wait_ge(s_x2, TILES)
            for i in range(TILES):
                pe.wait_ge(s_xh, TILES + i + 1)
                for j in range(J):
                    last = nc.tensor.transpose(bank[0][:, j * P:j * P + P], xh[:, i, j, :], ident[:, :])
                last.then_inc(s_T2, 1)
                pe.wait_ge(s_xhT2, i + 1)
                for j in range(J):
                    c = (J * i + j) * E
                    last = mm(bank[5][:, c:c + E], xhT[:, i, j, :], gateT_sb[:, :], start=True, stop=True)
            last.then_inc(s_g, 1)
            pe.wait_ge(s_free, 1)
            for i in range(TILES):
                if i:
                    pe.wait_ge(s_cTs, i)
                for j in range(J):
                    last = nc.tensor.transpose(bank[0][0:E, j * P:j * P + P], comb[:, J * i + j, :], ident[:, :])
                last.then_inc(s_cT, 1)
            pe.wait_ge(s_cTs, TILES)
            pe.wait_ge(s_w1, 16)
            pe.wait_ge(s_w2, 16)
            with pe.Fori(0, TILES) as i:
                for e in range(E):
                    mm(bank[4][:, :], esel[:, e, :], combT[:, bass.ds(i, 1), :].rearrange("e a n -> e (a n)"),
                       start=True, stop=True).then_inc(s_bc, 1)
                    for c in range(HC):
                        mm(bank[c][:, :], w1_sb[:, e, c * P:c * P + P],
                           xhT[:, bass.ds(i, 1), :, :].rearrange("d a j q -> d (a j q)"),
                           start=True, stop=True).then_inc(s_up, 1)
                    pe.wait_ge(s_free, E * i + e + 1)
                    for c in range(HC):
                        pe.wait_ge(s_h, HC * (E * i + e) + c + 1)
                        last = mm(bank[5][:, :], w2_sb[:, e, c, :], hsb[:, c, :], start=(c == 0), stop=(c == HC - 1))
                    last.then_inc(s_dn, 1)
                pe.wait_ge(s_add, (E - 1) * i + E - 1)
                for j in range(J):
                    last = nc.tensor.transpose(bank[6][:, j * P:j * P + P], acc[:, j * P:j * P + P], ident[:, :])
                last.then_inc(s_oT, 1)


def kernel(L0_attn_x, L0_attn_A, L0_attn_Bm, L0_attn_C, L0_attn_D, L0_attn_W_in, L0_attn_b_in,
           L0_ffn_gate_w, L0_ffn_w1, L0_ffn_b1, L0_ffn_w2, L0_ffn_b2):
    import numpy as np
    import concourse.bacc as bacc
    from concourse.bass_utils import run_bass_kernel_spmd

    a = [np.asarray(v) for v in (L0_attn_x, L0_attn_A, L0_attn_Bm, L0_attn_C, L0_attn_D, L0_attn_W_in, L0_attn_b_in,
                                 L0_ffn_gate_w, L0_ffn_w1, L0_ffn_b1, L0_ffn_w2, L0_ffn_b2)]
    x, A, Bm, C, Dv, W_in, b_in, gate_w, w1, b1, w2, b2 = a
    laid = {
        "x": x.reshape(TILES * J * P, D), "A": A, "AT": A.T, "BmT": Bm.T, "Bm": Bm, "CT": C.T, "Dv": Dv,
        "W_in": W_in, "b_in": b_in.reshape(N, 1), "gateT": gate_w.T,
        "w1T": w1.transpose(2, 0, 1),
        "b1": b1.reshape(E, HC, P).transpose(2, 0, 1).reshape(P, E * HC),
        "w2T": w2.transpose(0, 2, 1).reshape(E, HC, P, D).transpose(2, 0, 1, 3),
        "b2": b2.T,
    }
    laid = {k: np.ascontiguousarray(v) for k, v in laid.items()}
    nc = bacc.Bacc("TRN2", target_bir_lowering=False, num_devices=1)
    args = [nc.dram_tensor(k, v.shape, mybir.dt.float32, kind="ExternalInput").ap() for k, v in laid.items()]
    by = dict(zip(laid, args))
    out = nc.dram_tensor("out", (TILES * J * P, D), mybir.dt.float32, kind="ExternalOutput").ap()
    build(nc, by["x"], by["A"], by["AT"], by["BmT"], by["Bm"], by["CT"], by["Dv"], by["W_in"], by["b_in"],
          by["gateT"], by["w1T"], by["b1"], by["w2T"], by["b2"], out)
    r = run_bass_kernel_spmd(nc, [laid], core_ids=[0])
    return r.results[0]["out"].reshape(x.shape)
```

```python
import concourse.bass as bass
from concourse import mybir
from contextlib import ExitStack

FP32 = mybir.dt.float32
ALU = mybir.AluOpType
ACT = mybir.ActivationFunctionType
AX = mybir.AxisListType

P = 128
D = 128
N = 32
J = 4
TILES = 8
COLS = TILES * J
SEQ_CHUNKS = 64
SEQS = 2
G = 4
GT = TILES // G
DOUBLINGS = 6
E = 8
HID = 512
HC = HID // P
EPS = 1e-5
TOKENS = TILES * J * P
TOP = 2
B = 2 * P
UB = B // P
NB = (TOP * TOKENS + E * (B - 1)) // B
NU = NB * UB
ROW = D + E
WST = HID + HC * D + HC + 1
RING = 4
LOOPED = (NB - RING + 1) // RING * RING
HALF = TOKENS // 2
FP16 = mybir.dt.float16
BF16 = mybir.dt.bfloat16
I32 = mybir.dt.int32


def build(nc, x, A, AT, BmT, Bm, CT, Dv, W_in, b_in, gateT, wall, xg, out):
    ctx = ExitStack()
    with ctx:
        def sb(name, shape, dt=FP32):
            return ctx.enter_context(nc.sbuf_tensor(name, shape, dt))

        def sem(name):
            return ctx.enter_context(nc.semaphore(name))

        bank = [ctx.enter_context(nc.psum_tensor(f"bank{k}", [P, 512], FP32)) for k in range(8)]

        x_sb = sb("x_sb", [P, TILES, J, D])
        A_sb = sb("A_sb", [N, N])
        AT_sb = sb("AT_sb", [N, N])
        BmT_sb = sb("BmT_sb", [N, N])
        Bm_sb = sb("Bm_sb", [N, N])
        CT_sb = sb("CT_sb", [N, D])
        Win_sb = sb("Win_sb", [N, D])
        bin_sb = sb("bin_sb", [N, 1])
        Dbc = sb("Dbc", [P, D])
        gateT_sb = sb("gateT_sb", [D, E])
        w_sb = sb("w_sb", [P, E, WST])
        ident = sb("ident", [P, P])
        eiota = sb("eiota", [P, COLS, E])
        lower = sb("lower", [P, P], BF16)
        ones = sb("ones", [P, P], BF16)
        restart = sb("restart", [P, E, COLS])
        steps = sb("steps", [P, E, TOKENS // B])
        biota = sb("biota", [1, NB, E])
        riota = sb("riota", [P, P], FP16)
        uiota = sb("uiota", [P, NU], FP16)
        code = sb("code", [P, TOP * COLS])
        spare = sb("spare", [P, NB, UB])
        zrow = sb("zrow", [P, ROW])
        Apow = sb("Apow", [N, J + 1, N])
        ATpow = sb("ATpow", [N, J + 1, N])
        ATrep = sb("ATrep", [N, J + 1, G, N])
        sq = sb("sq", [N, DOUBLINGS, 2, N])
        sqrep = sb("sqrep", [N, DOUBLINGS, G, N])
        bd = sb("bd", [P, DOUBLINGS, P])
        Gst = sb("Gst", [D, (2 * J - 1) * N])
        Msum = sb("Msum", [N, J, N])
        v0 = sb("v0", [N, 1])
        BA = sb("BA", [N, P])
        hbias = sb("hbias", [P, 1])
        bdC = sb("bdC", [P, J, D])
        Rc = sb("Rc", [P, J, D])
        stats = sb("stats", [P, COLS, 6])
        mean = sb("mean", [P, COLS])
        var = sb("var", [P, COLS])
        sd = sb("sd", [P, COLS])
        rs = sb("rs", [P, COLS])
        tn = sb("tn", [P, COLS])
        xh = sb("xh", [P, TILES, J, ROW])
        xhT = sb("xhT", [D, TILES, J, P])
        hloc = sb("hloc", [P, TILES, P])
        ebuf = sb("ebuf", [P, GT * SEQS, SEQ_CHUNKS + 1])
        cbuf = sb("cbuf", [P, GT, P])
        lg = sb("lg", [P, COLS, E])
        ex = sb("ex", [P, COLS, E])
        pr = sb("pr", [P, COLS, E])
        oh = sb("oh", [P, TOP, COLS, E])
        both = sb("both", [P, COLS, E], BF16)
        r1 = sb("r1", [P, 6, COLS])
        tot = sb("tot", [P, E, COLS])
        upto = sb("upto", [P, E, COLS])
        cmp_ = sb("cmp_", [P, E, TOKENS // B])
        nblk = sb("nblk", [P, E])
        cum = sb("cum", [P, E])
        first = sb("first", [P, E])
        bcmp = sb("bcmp", [1, NB, E])
        bexp = sb("bexp", [1, NB])
        bexp_i = sb("bexp_i", [1, NB], I32)
        slot = sb("slot", [P, TOP * COLS])
        slot_i = sb("slot_i", [P, 3, TOP * COLS], I32)
        s_in = sb("s_in", [P, 2, TOP * COLS])
        R = sb("R", [P, TOP * COLS, P], FP16)
        O = sb("O", [P, TOP * COLS, NU], FP16)
        dc = sb("dc", [P, 2, NU])
        idx = sb("idx", [P, NU], I32)
        xr = sb("xr", [P, RING, UB, ROW])
        xgT = sb("xgT", [D, 2, B])
        wst = sb("wst", [P, 2, WST])
        hsb = sb("hsb", [P, HC, B])
        yT = sb("yT", [D, B])
        ys = sb("ys", [P, 2, UB, D])

        s_small = sem("s_small")
        s_x = [sem(f"s_x{i}") for i in range(2)]
        s_w = sem("s_w")
        s_const = sem("s_const")
        s_id = sem("s_id")
        s_pool = sem("s_pool")
        s_pe = sem("s_pe")
        s_v = sem("s_v")
        s_a = sem("s_a")
        s_set = sem("s_set")
        s_st = sem("s_st")
        s_var = sem("s_var")
        s_sd = sem("s_sd")
        s_xh = sem("s_xh")
        s_T = sem("s_T")
        s_xhT = sem("s_xhT")
        s_H = sem("s_H")
        s_hloc = sem("s_hloc")
        s_e = sem("s_e")
        s_sc = sem("s_sc")
        s_car = sem("s_car")
        s_y = sem("s_y")
        s_x2 = sem("s_x2")
        s_xd = sem("s_xd")
        s_T2 = sem("s_T2")
        s_xhT2 = sem("s_xhT2")
        s_g = sem("s_g")
        s_exp = sem("s_exp")
        s_lgm = sem("s_lgm")
        s_zero = sem("s_zero")
        s_both = sem("s_both")
        s_rank = sem("s_rank")
        s_share = sem("s_share")
        s_res = sem("s_res")
        s_rows = sem("s_rows")
        s_RO = sem("s_RO")
        s_idx = sem("s_idx")
        s_be = sem("s_be")
        s_dec = sem("s_dec")
        s_gat = [sem(f"s_gat{k}") for k in range(RING)]
        s_tx = sem("s_tx")
        s_xgT = sem("s_xgT")
        s_wst = sem("s_wst")
        s_up = sem("s_up")
        s_h = sem("s_h")
        s_dn = sem("s_dn")
        s_yT = sem("s_yT")
        s_ot = sem("s_ot")
        s_ys = sem("s_ys")
        s_sca = [sem(f"s_sca{k}") for k in range(2)]

        block = ctx.enter_context(nc.Block())
        x_v = x.rearrange("(i q j) d -> i q (j d)", q=P, j=J)
        out_v = out[0:TOKENS, :].rearrange("(i q j) d -> i q (j d)", q=P, j=J)
        xg_v = xg[0:TOKENS, :].rearrange("(i q j) w -> i q j w", q=P, j=J)
        CONSTS = 3 + 6 + 2 * TOP + 2
        SMALL = 9 + G

        def scattered(k, turn=0):
            return 16 * UB * (turn * (RING // 2) + k // 2 + 2)

        @block.sync
        def _(sp):
            for h in range(2):
                sp.dma_start(x_sb[:, 4 * h:4 * h + 4, :, :].rearrange("q i j d -> q i (j d)"),
                             x_v[4 * h:4 * h + 4].rearrange("i q n -> q i n")).then_inc(s_x[h], 16)
            sp.dma_start(w_sb[:, :, :], wall).then_inc(s_w, 16)
            with sp.Fori(0, TILES) as i:
                sp.wait_ge(s_x2, i + 1)
                sp.dma_start(out_v[bass.ds(i, 1)].rearrange("a q n -> q (a n)"),
                             x_sb[:, bass.ds(i, 1), :, :].rearrange("q a j d -> q (a j d)")).then_inc(s_res, 16)
            with sp.Fori(0, TILES) as i:
                sp.wait_ge(s_xh, TILES + i + 1)
                sp.dma_start(xg_v[bass.ds(i, 1), :, :, 0:D].rearrange("a q j d -> q (a j) d"),
                             xh[:, bass.ds(i, 1), :, 0:D].rearrange("q a j d -> q (a j) d")).then_inc(s_rows, 16)
            sp.wait_ge(s_share, 1)
            for i in range(TILES):
                sp.dma_start(xg_v[i, :, :, D:ROW], xh[:, i, :, D:ROW]).then_inc(s_rows, 16)

        @block.gpsimd
        def _(pool):
            nc.gpsimd.memset(ident[:], 0.0).then_inc(s_id, 1)
            nc.gpsimd.memset(bdC[:], 0.0).then_inc(s_id, 1)
            pool.wait_ge(s_id, 2)
            nc.gpsimd.affine_select(out=ident[:], in_=ident[:], compare_op=ALU.not_equal, fill=1.0, base=0,
                                    pattern=[[-1, P]], channel_multiplier=1).then_inc(s_pool, 1)
            nc.gpsimd.memset(zrow[:], 0.0).then_inc(s_zero, 1)
            pool.wait_ge(s_zero, 1)
            for u in range(UB):
                past = TOKENS + P * u
                nc.gpsimd.dma_start(out[past:past + P, :], zrow[:, 0:D]).then_inc(s_sca[0], 16)
                nc.gpsimd.dma_start(xg[past:past + P, :], zrow[:, :]).then_inc(s_sca[1], 16)
            nc.gpsimd.memset(ones[:], 1.0).then_inc(s_const, 1)
            nc.gpsimd.memset(lower[:], 1.0).then_inc(s_const, 1)
            nc.gpsimd.memset(restart[:], 1.0).then_inc(s_const, 1)

            def count(dst, pattern, base=0, q=0):
                nc.gpsimd.iota(dst, pattern, base=base, channel_multiplier=q,
                               allow_small_or_imprecise_dtypes=True).then_inc(s_const, 1)

            count(eiota[:], [[0, COLS], [-1, E]], base=E)
            count(steps[:], [[0, E], [B, TOKENS // B]])
            count(biota[:], [[1, NB], [0, E]])
            count(riota[:], [[1, P]])
            count(uiota[:], [[1, NU]])
            for m in range(2 * TOP):
                count(code[:, m * COLS // 2:(m + 1) * COLS // 2], [[J * P, TILES // 2], [1, J]],
                      base=1 if m % 2 else -HALF, q=J)
            count(spare[:], [[0, NB], [P, UB]], base=TOKENS - HALF, q=1)
            pool.wait_ge(s_const, 3)
            nc.gpsimd.affine_select(out=lower[:], in_=lower[:], compare_op=ALU.is_gt, fill=0.0, base=0,
                                    pattern=[[1, P]], channel_multiplier=-1).then_inc(s_const, 1)
            nc.gpsimd.affine_select(out=restart[:], in_=restart[:], compare_op=ALU.not_equal, fill=0.0, base=0,
                                    pattern=[[0, E], [1, COLS]], channel_multiplier=0).then_inc(s_const, 1)
            pool.wait_ge(s_small, 16 * SMALL)
            with pool.Fori(0, TILES) as i:
                for h in range(2):
                    pool.wait_ge(s_x[h], 16)
                pool.wait_ge(s_xh, i + 1)
                nc.gpsimd.tensor_tensor(x_sb[:, i, :, :], x_sb[:, i, :, :],
                                        Dbc[:, :].unsqueeze(1).to_broadcast([P, J, D]), ALU.add).then_inc(s_xd, 1)

            def gather(b):
                if b >= RING:
                    pool.wait_ge(s_ys, b - RING + 1)
                for u in range(UB):
                    nc.gpsimd.indirect_dma_start(
                        out=xr[:, b % RING, u, :], out_offset=None, in_=xg,
                        in_offset=bass.IndirectOffsetOnAxis(ap=idx[:, UB * b + u:UB * b + u + 1], axis=0),
                    ).then_inc(s_gat[b % RING], 16)

            def scatter(b):
                pool.wait_ge(s_ys, b + 1)
                pool.wait_ge(s_sca[(b + 1) % 2], scattered(b - 1))
                for u in range(UB):
                    nc.gpsimd.indirect_dma_start(
                        out=out, in_=ys[:, b % 2, u, :], in_offset=None, compute_op=ALU.add,
                        out_offset=bass.IndirectOffsetOnAxis(ap=idx[:, UB * b + u:UB * b + u + 1], axis=0),
                    ).then_inc(s_sca[b % 2], 16)

            pool.wait_ge(s_dec, 1)
            pool.wait_ge(s_rows, 16 * 2 * TILES)
            pool.wait_ge(s_sca[1], 16 * UB)
            for b in range(RING - 1):
                gather(b)
            pool.wait_ge(s_res, 16 * TILES)
            for b in range(NB):
                if b + RING - 1 < NB:
                    gather(b + RING - 1)
                scatter(b)
            for b in (NB - 2, NB - 1):
                pool.wait_ge(s_sca[b % 2], scattered(b))

        @block.scalar
        def _(act):
            for dst, src in ((A_sb, A), (AT_sb, AT), (BmT_sb, BmT), (Bm_sb, Bm), (CT_sb, CT), (Win_sb, W_in),
                             (bin_sb, b_in), (gateT_sb, gateT)):
                act.dma_start(dst[:, :], src).then_inc(s_small, 16)
            act.dma_start(Dbc[:, :], Dv.rearrange("(a d) -> a d", a=1).to_broadcast([P, D])).then_inc(s_small, 16)
            act.wait_ge(s_id, 2)
            for g in range(G):
                act.dma_start(bdC[N * g:N * g + N, g, :], CT).then_inc(s_small, 16)

            def root(layer):
                act.wait_ge(s_var, layer + 1)
                nc.scalar.activation(sd[:, :], var[:, :], ACT.Sqrt).then_inc(s_sd, 1)

            root(0)
            with act.Fori(0, TILES) as i:
                act.wait_ge(s_T, i + 1)
                nc.scalar.activation(xhT[:, i, :, :], bank[0][:, :], ACT.Identity).then_inc(s_xhT, 1)
                act.wait_ge(s_H, i + 1)
                nc.scalar.activation(hloc[:, i, :], bank[1][:, 0:P], ACT.Identity,
                                     bias=hbias[:, :]).then_inc(s_hloc, 1)
            root(1)
            with act.Fori(0, TILES) as i:
                act.wait_ge(s_T2, i + 1)
                nc.scalar.activation(xhT[:, i, :, :], bank[0][:, :], ACT.Identity).then_inc(s_xhT2, 1)
            act.wait_ge(s_lgm, 1)
            nc.scalar.activation(ex[:, :, :], lg[:, :, :], ACT.Exp).then_inc(s_exp, 1)

            def stage(b, k):
                e = nc.scalar.value_load(bexp_i[0:1, bass.ds(b, 1)], min_val=0, max_val=E - 1)
                nc.scalar.activation(wst[:, k % 2, :], w_sb[:, bass.ds(e, 1), :].rearrange("p a n -> p (a n)"),
                                     ACT.Identity).then_inc(s_wst, 1)

            def hidden(b, k):
                for c in range(HC):
                    act.wait_ge(s_up, HC * b + c + 1)
                    nc.scalar.activation(hsb[:, c, :], bank[c][:, 0:B], ACT.Relu,
                                         bias=wst[:, k % 2, WST - 1 - HC + c:WST - HC + c]).then_inc(s_h, 1)

            act.wait_ge(s_w, 16)
            act.wait_ge(s_be, 1)
            stage(0, 0)
            stage(1, 1)
            act.wait_ge(s_wst, 2)
            hidden(0, 0)
            with act.Fori(0, LOOPED // RING) as turn:
                for k in range(RING):
                    b = RING * turn + k
                    hidden(b + 1, k + 1)
                    act.wait_ge(s_yT, b + 1)
                    stage(b + 2, k)
                    act.wait_ge(s_wst, b + 3)
            for b in range(LOOPED, NB):
                if b + 1 < NB:
                    hidden(b + 1, b + 1)
                if b + 2 < NB:
                    act.wait_ge(s_yT, b + 1)
                    stage(b + 2, b)
                    act.wait_ge(s_wst, b + 3)

        @block.vector
        def _(dve):
            chain = [0]

            def link(ins):
                chain[0] += 1
                ins.then_inc(s_v, 1)
                dve.wait_ge(s_v, chain[0])

            nc.vector.memset(Gst[:], 0.0)
            nc.vector.memset(bd[:], 0.0)
            link(nc.vector.memset(ebuf[:], 0.0))

            dve.wait_ge(s_small, 16 * SMALL)
            dve.wait_ge(s_pool, 1)
            nc.vector.tensor_copy(Apow[:, 0, :], ident[0:N, 0:N])
            nc.vector.tensor_copy(ATpow[:, 0, :], ident[0:N, 0:N])
            nc.vector.tensor_copy(Apow[:, 1, :], A_sb[:, :])
            nc.vector.tensor_copy(ATpow[:, 1, :], AT_sb[:, :]).then_inc(s_set, 1)
            S = bank[7]
            dve.wait_ge(s_pe, 1)
            nc.vector.tensor_copy(v0[:, :], bank[5][0:N, 0:1])
            for k in range(2, J + 1):
                dve.wait_ge(s_pe, k)
                nc.vector.tensor_copy(Apow[:, k, :], S[0:N, 0:N])
                nc.vector.tensor_copy(ATpow[:, k, :], S[0:N, N:2 * N]).then_inc(s_set, 1)
            link(nc.vector.tensor_copy(sq[:, 0, :, :].rearrange("n a m -> n (a m)"), S[0:N, 0:2 * N]))
            for k in range(J + 1):
                nc.vector.tensor_copy(ATrep[:, k, :, :], ATpow[:, k, :].unsqueeze(1).to_broadcast([N, G, N]))
            nc.vector.tensor_copy(Msum[:, 0, :], Apow[:, 0, :])
            link(nc.vector.tensor_tensor(Msum[:, 1, :], Apow[:, 0, :], Apow[:, 1, :], ALU.add))
            link(nc.vector.tensor_tensor(Msum[:, 2, :], Msum[:, 1, :], Apow[:, 2, :], ALU.add))
            nc.vector.tensor_tensor(Msum[:, 3, :], Msum[:, 2, :], Apow[:, 3, :], ALU.add).then_inc(s_set, 1)
            for k in range(DOUBLINGS):
                nc.vector.tensor_copy(sqrep[:, k, :, :],
                                      sq[:, k, 1, :].unsqueeze(1).to_broadcast([N, G, N])).then_inc(s_set, 1)
                dve.wait_ge(s_pe, J + 1 + k)
                if k < DOUBLINGS - 1:
                    nc.vector.tensor_copy(sq[:, k + 1, :, :].rearrange("n a m -> n (a m)"), S[0:N, 0:2 * N])
                for g in range(G):
                    last = nc.vector.tensor_copy(bd[N * g:N * g + N, k, N * g:N * g + N],
                                                 S[N * g:N * g + N, 2 * N:3 * N])
                if k < DOUBLINGS - 1:
                    link(last)
                else:
                    last.then_inc(s_set, 1)
            dve.wait_ge(s_pe, J + 1 + DOUBLINGS)
            nc.vector.tensor_copy(BA[:, :], S[0:N, 0:P]).then_inc(s_set, 1)
            dve.wait_ge(s_pe, J + 2 + DOUBLINGS)
            nc.vector.tensor_copy(Gst[:, (J - 1) * N:(2 * J - 1) * N], S[:, 0:J * N])
            nc.vector.tensor_copy(hbias[:, :], S[:, J * N:J * N + 1]).then_inc(s_set, 1)
            dve.wait_ge(s_pe, J + 3 + DOUBLINGS)
            nc.vector.tensor_copy(Rc[:, :, :].rearrange("n j d -> n (j d)"), bank[6][:, :]).then_inc(s_set, 1)

            def statistics(i, src):
                for j in range(J):
                    last = nc.vector.bn_stats(stats[:, bass.ds(J * i + j, 1), :].rearrange("p a s -> p (a s)"),
                                              src[:, i, j, :])
                last.then_inc(s_st, 1)

            def moments(layer):
                dve.wait_ge(s_st, TILES * (layer + 1))
                nc.vector.tensor_tensor(mean[:, :], stats[:, :, 1], stats[:, :, 4], ALU.add)
                nc.vector.tensor_tensor(tn[:, :], stats[:, :, 1], stats[:, :, 4], ALU.subtract)
                link(nc.vector.tensor_tensor(var[:, :], stats[:, :, 2], stats[:, :, 5], ALU.add))
                nc.vector.tensor_scalar(mean[:, :], mean[:, :], 0.5, None, ALU.mult)
                link(nc.vector.tensor_tensor(tn[:, :], tn[:, :], tn[:, :], ALU.mult))
                link(nc.vector.tensor_scalar(tn[:, :], tn[:, :], 0.25, EPS, ALU.mult, ALU.add))
                nc.vector.scalar_tensor_tensor(var[:, :], var[:, :], 1.0 / D, tn[:, :],
                                               ALU.mult, ALU.add).then_inc(s_var, 1)
                dve.wait_ge(s_sd, layer + 1)
                link(nc.vector.reciprocal(rs[:, :], sd[:, :]))
                link(nc.vector.tensor_tensor(tn[:, :], rs[:, :], rs[:, :], ALU.mult))
                link(nc.vector.tensor_tensor(tn[:, :], tn[:, :], var[:, :], ALU.mult))
                link(nc.vector.tensor_scalar(tn[:, :], tn[:, :], -0.5, 1.5, ALU.mult, ALU.add))
                link(nc.vector.tensor_tensor(rs[:, :], rs[:, :], tn[:, :], ALU.mult))

            def normalise(i, src):
                for j in range(J):
                    last = nc.vector.tensor_scalar(xh[:, i, j, 0:D], src[:, i, j, :],
                                                   mean[:, bass.ds(J * i + j, 1)], rs[:, bass.ds(J * i + j, 1)],
                                                   ALU.subtract, ALU.mult)
                last.then_inc(s_xh, 1)

            for h in range(2):
                dve.wait_ge(s_x[h], 16)
            with dve.Fori(0, TILES) as i:
                statistics(i, x_sb)
            moments(0)
            with dve.Fori(0, TILES) as i:
                normalise(i, x_sb)

            dve.wait_ge(s_hloc, TILES)
            for g in range(G):
                last = nc.vector.tensor_copy(
                    ebuf[N * g:N * g + N, :, 1:],
                    hloc[P - N:P, GT * g:GT * g + GT, :].rearrange("n t (s c) -> n (t s) c", s=SEQS))
            last.then_inc(s_e, 1)
            for k in range(DOUBLINGS):
                step = 1 << k
                dve.wait_ge(s_sc, k + 1)
                dve.wait_ge(s_e, k + 1)
                nc.vector.tensor_tensor(
                    ebuf[:, :, 1 + step:], ebuf[:, :, 1 + step:],
                    bank[2][:, 0:GT * P].rearrange("n (s c) -> n s c", c=SEQ_CHUNKS)[:, :, 0:SEQ_CHUNKS - step],
                    ALU.add).then_inc(s_e, 1)
            dve.wait_ge(s_e, DOUBLINGS + 1)
            nc.vector.tensor_copy(cbuf[:, :, :].rearrange("n t (s c) -> n (t s) c", s=SEQS),
                                  ebuf[:, :, 0:SEQ_CHUNKS]).then_inc(s_car, 1)

            dve.wait_ge(s_xd, TILES)
            for i in range(TILES):
                dve.wait_ge(s_y, i + 1)
                x_tile = x_sb[:, i, :, :].rearrange("q j d -> q (j d)")
                nc.vector.tensor_tensor(x_tile, x_tile, bank[i % 2][:, :], ALU.add).then_inc(s_x2, 1)
                dve.wait_ge(s_x2, i + 1)
                statistics(i, x_sb)
            moments(1)
            with dve.Fori(0, TILES) as i:
                normalise(i, x_sb)

            dve.wait_ge(s_const, CONSTS)
            dve.wait_ge(s_g, 1)

            def wide(a, n=E):
                return a.unsqueeze(2).to_broadcast([P, a.shape[1], n])

            G3 = bank[5][:, 0:COLS * E].rearrange("p (t e) -> p t e", e=E)
            link(nc.vector.tensor_reduce(r1[:, 0, :], G3, AX.X, ALU.max))
            nc.vector.tensor_tensor(lg[:, :, :], G3, wide(r1[:, 0, :]), ALU.subtract).then_inc(s_lgm, 1)
            dve.wait_ge(s_lgm, 1)
            link(nc.vector.scalar_tensor_tensor(pr[:, :, :], lg[:, :, :], 0.0, eiota[:, :, :],
                                                ALU.is_equal, ALU.mult))
            link(nc.vector.tensor_reduce(r1[:, 1, :], pr[:, :, :], AX.X, ALU.max))
            link(nc.vector.tensor_tensor(oh[:, 0, :, :], eiota[:, :, :], wide(r1[:, 1, :]), ALU.is_equal))
            link(nc.vector.scalar_tensor_tensor(pr[:, :, :], oh[:, 0, :, :], -3e38, lg[:, :, :], ALU.mult, ALU.add))
            link(nc.vector.tensor_reduce(r1[:, 2, :], pr[:, :, :], AX.X, ALU.max))
            link(nc.vector.tensor_tensor(pr[:, :, :], pr[:, :, :], wide(r1[:, 2, :]), ALU.is_equal))
            link(nc.vector.tensor_tensor(pr[:, :, :], pr[:, :, :], eiota[:, :, :], ALU.mult))
            link(nc.vector.tensor_reduce(r1[:, 3, :], pr[:, :, :], AX.X, ALU.max))
            link(nc.vector.tensor_tensor(oh[:, 1, :, :], eiota[:, :, :], wide(r1[:, 3, :]), ALU.is_equal))
            nc.vector.tensor_tensor(both[:, :, :], oh[:, 0, :, :], oh[:, 1, :, :], ALU.add).then_inc(s_both, 1)
            dve.wait_ge(s_exp, 1)
            link(nc.vector.tensor_reduce(r1[:, 4, :], ex[:, :, :], AX.X, ALU.add))
            link(nc.vector.reciprocal(r1[:, 4, :], r1[:, 4, :]))
            dve.wait_ge(s_both, 1)
            link(nc.vector.tensor_tensor(pr[:, :, :], ex[:, :, :], wide(r1[:, 4, :]), ALU.mult))
            link(nc.vector.tensor_tensor(pr[:, :, :], pr[:, :, :], both[:, :, :], ALU.mult))
            link(nc.vector.tensor_reduce(r1[:, 4, :], pr[:, :, :], AX.X, ALU.add))
            link(nc.vector.reciprocal(r1[:, 4, :], r1[:, 4, :]))
            nc.vector.tensor_tensor(xh[:, :, :, D:ROW].rearrange("q i j e -> q (i j) e"), pr[:, :, :],
                                    wide(r1[:, 4, :]), ALU.mult).then_inc(s_share, 1)

            dve.wait_ge(s_rank, 1)
            link(nc.vector.tensor_copy(tot[:, :, :], bank[7][:, 0:COLS * E].rearrange("p (t e) -> p e t", e=E)))
            link(nc.vector.tensor_tensor_scan(upto[:, :, :].rearrange("p e t -> p (e t)"),
                                              restart[:, :, :].rearrange("p e t -> p (e t)"),
                                              tot[:, :, :].rearrange("p e t -> p (e t)"), 0.0, ALU.mult, ALU.add))
            nc.vector.tensor_tensor(tot[:, :, :], upto[:, :, :], tot[:, :, :], ALU.subtract)
            link(nc.vector.tensor_tensor(cmp_[:, :, :], wide(upto[:, :, COLS - 1], TOKENS // B), steps[:, :, :],
                                         ALU.is_gt))
            link(nc.vector.tensor_reduce(nblk[:, :], cmp_[:, :, :], AX.X, ALU.add))
            link(nc.vector.tensor_tensor_scan(cum[:, :], ones[:, 0:E], nblk[:, :], 0.0, ALU.mult, ALU.add))
            link(nc.vector.tensor_tensor(first[:, :], cum[:, :], nblk[:, :], ALU.subtract))
            nc.vector.tensor_tensor(bcmp[:, :, :], biota[:, :, :], cum[0:1, :].unsqueeze(1).to_broadcast([1, NB, E]),
                                    ALU.is_ge)
            link(nc.vector.scalar_tensor_tensor(tot[:, :, :], wide(first[:, :], COLS), float(B), tot[:, :, :],
                                                ALU.mult, ALU.add))
            link(nc.vector.tensor_reduce(bexp[:, :], bcmp[:, :, :], AX.X, ALU.add))
            nc.vector.tensor_scalar(bexp_i[:, :], bexp[:, :], float(E - 1), None, ALU.min).then_inc(s_be, 1)
            link(nc.vector.tensor_tensor(lg[:, :, :], bank[6][:, 0:COLS * E].rearrange("p (t e) -> p t e", e=E),
                                         tot[:, :, :].rearrange("p e t -> p t e"), ALU.add))
            for k in range(TOP):
                link(nc.vector.tensor_tensor(oh[:, k, :, :], oh[:, k, :, :], lg[:, :, :], ALU.mult))
            link(nc.vector.tensor_reduce(slot[:, :], oh[:, :, :, :].rearrange("p k t e -> p (k t) e"), AX.X, ALU.add))
            link(nc.vector.tensor_copy(slot_i[:, 0, :], slot[:, :]))
            nc.vector.tensor_scalar(slot_i[:, 1, :], slot_i[:, 0, :], P - 1, None, ALU.bitwise_and)
            link(nc.vector.tensor_scalar(slot_i[:, 2, :], slot_i[:, 0, :], P.bit_length() - 1, None,
                                         ALU.logical_shift_right))
            link(nc.vector.tensor_copy(s_in[:, :, :], slot_i[:, 1:3, :]))

            with dve.Fori(0, TOP * COLS // 8) as t:
                for m in range(8):
                    n = 8 * t + m
                    nc.vector.tensor_scalar(R[:, bass.ds(n, 1), :].rearrange("p a r -> p (a r)"), riota[:, :],
                                            s_in[:, 0, bass.ds(n, 1)], None, ALU.is_equal)
                    last = nc.vector.tensor_scalar(O[:, bass.ds(n, 1), :].rearrange("p a u -> p (a u)"), uiota[:, :],
                                                   s_in[:, 1, bass.ds(n, 1)], code[:, bass.ds(n, 1)],
                                                   ALU.is_equal, ALU.mult)
                last.then_inc(s_RO, 1)
            dve.wait_ge(s_idx, 1)
            a = bank[4][:, 0:NU]
            nc.vector.scalar_tensor_tensor(dc[:, 1, :], a, 0.0, spare[:, :, :].rearrange("p b u -> p (b u)"),
                                           ALU.is_equal, ALU.mult)
            link(nc.vector.tensor_scalar(dc[:, 0, :], a, 0.0, -1.0, ALU.is_gt, ALU.mult))
            link(nc.vector.scalar_tensor_tensor(dc[:, 0, :], a, float(HALF), dc[:, 0, :], ALU.add, ALU.add))
            nc.vector.tensor_tensor(idx[:, :], dc[:, 0, :], dc[:, 1, :], ALU.add).then_inc(s_dec, 1)

            def rows_in(b, k):
                dve.wait_ge(s_tx, b + 1)
                nc.vector.tensor_copy(xgT[:, k % 2, :], bank[6][:, 0:B]).then_inc(s_xgT, 1)

            def rows_out(turn, k):
                b = RING * turn + k
                dve.wait_ge(s_dn, b + 1)
                nc.vector.tensor_scalar(yT[:, :], bank[4][:, 0:B], wst[:, k % 2, WST - 1:WST], None,
                                        ALU.add).then_inc(s_yT, 1)
                e = nc.vector.value_load(bexp_i[0:1, bass.ds(b, 1)], min_val=0, max_val=E - 1)
                dve.wait_ge(s_ot, b + 1)
                dve.wait_ge(s_sca[k % 2], scattered(k - 2, turn))
                for u in range(UB):
                    last = nc.vector.tensor_scalar(ys[:, k % 2, u, :], bank[5][:, u * P:u * P + P],
                                                   xr[:, k, u, bass.ds(e + D, 1)], None, ALU.mult)
                last.then_inc(s_ys, 1)

            dve.wait_ge(s_wst, 2)
            rows_in(0, 0)
            rows_in(1, 1)
            with dve.Fori(0, LOOPED // RING) as turn:
                for k in range(RING):
                    b = RING * turn + k
                    rows_out(turn, k)
                    rows_in(b + 2, k)
            for b in range(LOOPED, NB):
                turn, k = b // RING, b % RING
                rows_out(turn, k)
                if b + 2 < NB:
                    rows_in(b + 2, k)

        @block.tensor
        def _(pe):
            S = bank[7]
            mm = nc.tensor.matmul
            pe.wait_ge(s_small, 16 * SMALL)
            pe.wait_ge(s_pool, 1)
            pe.wait_ge(s_set, 1)
            mm(bank[5][0:N, 0:1], BmT_sb[:, :], bin_sb[:, :], start=True, stop=True).then_inc(s_pe, 1)
            for k in range(2, J + 1):
                pe.wait_ge(s_set, k - 1)
                mm(S[0:N, 0:N], AT_sb[:, :], Apow[:, k - 1, :], start=True, stop=True)
                mm(S[0:N, N:2 * N], A_sb[:, :], ATpow[:, k - 1, :], start=True, stop=True).then_inc(s_pe, 1)
            for k in range(DOUBLINGS):
                pe.wait_ge(s_set, J + 2 + k)
                mm(S[0:N, 0:N], sq[:, k, 1, :], sq[:, k, 0, :], start=True, stop=True)
                mm(S[0:N, N:2 * N], sq[:, k, 0, :], sq[:, k, 1, :], start=True, stop=True)
                mm(S[:, 2 * N:3 * N], sqrep[:, k, :, :].rearrange("n g m -> n (g m)"), ident[0:N, 0:N],
                   start=True, stop=True).then_inc(s_pe, 1)
            base = J + 1 + DOUBLINGS
            pe.wait_ge(s_set, base + 1)
            mm(S[0:N, 0:P], Bm_sb[:, :], Apow[:, 0:J, :].rearrange("n j m -> n (j m)"),
               start=True, stop=True).then_inc(s_pe, 1)
            pe.wait_ge(s_set, base + 2)
            mm(S[:, 0:P], Win_sb[:, :], BA[:, :], start=True, stop=True)
            mm(S[:, P:P + 1], Msum[:, :, :].rearrange("n j m -> n (j m)"), v0[:, :],
               start=True, stop=True).then_inc(s_pe, 1)
            for j in range(J):
                last = mm(bank[6][:, j * D:j * D + D], ATrep[:, j + 1, :, :].rearrange("n g m -> n (g m)"),
                          CT_sb[:, :], start=True, stop=True)
            last.then_inc(s_pe, 1)
            pe.wait_ge(s_set, base + 4)

            for i in range(TILES):
                pe.wait_ge(s_xh, i + 1)
                for j in range(J):
                    last = nc.tensor.transpose(bank[0][:, j * P:j * P + P], xh[:, i, j, 0:D], ident[:, :])
                last.then_inc(s_T, 1)
                pe.wait_ge(s_xhT, i + 1)
                for j in range(J):
                    last = mm(bank[1][:, 0:P], Gst[:, (J - 1 - j) * N:(2 * J - 1 - j) * N], xhT[:, i, j, :],
                              start=(j == 0), stop=(j == J - 1))
                last.then_inc(s_H, 1)

            for k in range(DOUBLINGS):
                pe.wait_ge(s_e, k + 1)
                mm(bank[2][:, 0:GT * P].rearrange("n (s c) -> n s c", c=SEQ_CHUNKS), bd[:, k, :], ebuf[:, :, 1:],
                   start=True, stop=True).then_inc(s_sc, 1)

            pe.wait_ge(s_car, 1)
            for i in range(TILES):
                g = i // GT
                if i >= 2:
                    pe.wait_ge(s_x2, i - 1)
                mm(bank[i % 2][:, :], hloc[:, i, :], bdC[:, :, :].rearrange("n j d -> n (j d)"),
                   start=True, stop=False)
                mm(bank[i % 2][:, :], cbuf[N * g:N * g + N, i % GT, :],
                   Rc[N * g:N * g + N, :, :].rearrange("n j d -> n (j d)"), start=False, stop=True).then_inc(s_y, 1)
            pe.wait_ge(s_x2, TILES)
            for i in range(TILES):
                pe.wait_ge(s_xh, TILES + i + 1)
                for j in range(J):
                    last = nc.tensor.transpose(bank[0][:, j * P:j * P + P], xh[:, i, j, 0:D], ident[:, :])
                last.then_inc(s_T2, 1)
                pe.wait_ge(s_xhT2, i + 1)
                for j in range(J):
                    c = (J * i + j) * E
                    last = mm(bank[5][:, c:c + E], xhT[:, i, j, :], gateT_sb[:, :], start=True, stop=True)
            last.then_inc(s_g, 1)
            pe.wait_ge(s_const, CONSTS)
            pe.wait_ge(s_both, 1)
            mm(bank[6][:, 0:COLS * E], lower[:, :], both[:, :, :].rearrange("p t e -> p (t e)"), start=True, stop=True)
            mm(bank[7][:, 0:COLS * E], ones[:, :], both[:, :, :].rearrange("p t e -> p (t e)"),
               start=True, stop=True).then_inc(s_rank, 1)
            for n in range(TOP * COLS):
                if n % 8 == 0:
                    pe.wait_ge(s_RO, n // 8 + 1)
                last = mm(bank[4][:, 0:NU], R[:, n, :], O[:, n, :], start=(n == 0), stop=(n == TOP * COLS - 1))
            last.then_inc(s_idx, 1)

            def rows_in(turn, k):
                pe.wait_ge(s_gat[k], 16 * UB * (turn + 1))
                for u in range(UB):
                    last = nc.tensor.transpose(bank[6][:, u * P:u * P + P], xr[:, k, u, 0:D], ident[:, :])
                last.then_inc(s_tx, 1)

            def up(b, k):
                pe.wait_ge(s_wst, b + 1)
                pe.wait_ge(s_xgT, b + 1)
                for c in range(HC):
                    mm(bank[c][:, 0:B], wst[:, k % 2, c * P:c * P + P], xgT[:, k % 2, :],
                       start=True, stop=True).then_inc(s_up, 1)

            def down(b, k):
                for c in range(HC):
                    pe.wait_ge(s_h, HC * b + c + 1)
                    last = mm(bank[4][:, 0:B], wst[:, k % 2, HID + c * D:HID + c * D + D], hsb[:, c, :],
                              start=(c == 0), stop=(c == HC - 1))
                last.then_inc(s_dn, 1)

            def rows_out(b):
                pe.wait_ge(s_yT, b + 1)
                for u in range(UB):
                    last = nc.tensor.transpose(bank[5][:, u * P:u * P + P], yT[:, u * P:u * P + P], ident[:, :])
                last.then_inc(s_ot, 1)

            rows_in(0, 0)
            pe.wait_ge(s_xgT, 1)
            rows_in(0, 1)
            up(0, 0)
            down(0, 0)
            with pe.Fori(0, LOOPED // RING) as turn:
                for k in range(RING):
                    b = RING * turn + k
                    up(b + 1, k + 1)
                    rows_out(b)
                    rows_in(turn + (k + 2) // RING, (k + 2) % RING)
                    down(b + 1, k + 1)
            for b in range(LOOPED, NB):
                if b + 1 < NB:
                    up(b + 1, b + 1)
                rows_out(b)
                if b + 2 < NB:
                    rows_in((b + 2) // RING, (b + 2) % RING)
                if b + 1 < NB:
                    down(b + 1, b + 1)


def kernel(L0_attn_x, L0_attn_A, L0_attn_Bm, L0_attn_C, L0_attn_D, L0_attn_W_in, L0_attn_b_in,
           L0_ffn_gate_w, L0_ffn_w1, L0_ffn_b1, L0_ffn_w2, L0_ffn_b2):
    import numpy as np
    import concourse.bacc as bacc
    from concourse.bass_utils import run_bass_kernel_spmd

    a = [np.asarray(v) for v in (L0_attn_x, L0_attn_A, L0_attn_Bm, L0_attn_C, L0_attn_D, L0_attn_W_in, L0_attn_b_in,
                                 L0_ffn_gate_w, L0_ffn_w1, L0_ffn_b1, L0_ffn_w2, L0_ffn_b2)]
    x, A, Bm, C, Dv, W_in, b_in, gate_w, w1, b1, w2, b2 = a
    laid = {
        "x": x.reshape(TILES * J * P, D), "A": A, "AT": A.T, "BmT": Bm.T, "Bm": Bm, "CT": C.T, "Dv": Dv,
        "W_in": W_in, "b_in": b_in.reshape(N, 1), "gateT": gate_w.T,
        "wall": np.concatenate([w1.transpose(2, 0, 1),
                                w2.transpose(0, 2, 1).reshape(E, HC, P, D).transpose(2, 0, 1, 3).reshape(P, E, HC * D),
                                b1.reshape(E, HC, P).transpose(2, 0, 1), b2.T.reshape(D, E, 1)], axis=2),
    }
    laid = {k: np.ascontiguousarray(v) for k, v in laid.items()}
    nc = bacc.Bacc("TRN2", target_bir_lowering=False, num_devices=1)
    args = [nc.dram_tensor(k, v.shape, mybir.dt.float32, kind="ExternalInput").ap() for k, v in laid.items()]
    by = dict(zip(laid, args))
    out = nc.dram_tensor("out", (TOKENS + B, D), mybir.dt.float32, kind="ExternalOutput").ap()
    xg = nc.dram_tensor("xg", (TOKENS + B, ROW), mybir.dt.float32, kind="Internal").ap()
    build(nc, by["x"], by["A"], by["AT"], by["BmT"], by["Bm"], by["CT"], by["Dv"], by["W_in"], by["b_in"],
          by["gateT"], by["wall"], xg, out)
    r = run_bass_kernel_spmd(nc, [laid], core_ids=[0])
    return r.results[0]["out"][0:TOKENS].reshape(x.shape)
```

```python
import concourse.bass as bass
from concourse import mybir
from contextlib import ExitStack

FP32 = mybir.dt.float32
ALU = mybir.AluOpType
ACT = mybir.ActivationFunctionType
AX = mybir.AxisListType

P = 128
D = 128
N = 32
J = 4
TILES = 8
COLS = TILES * J
SEQ_CHUNKS = 64
SEQS = 2
GE = 32
G = 4
DOUBLINGS = 6
E = 8
HID = 512
HC = HID // P
EPS = 1e-5
HALVES = 2
HT = TILES // HALVES
CARRYBANK = 1
SCANBANK = (4, 5)
YBANKS = (6, 7, 4)
GATEBANK = (5, 7)
TOKENS = TILES * J * P
TOP = 2
B = 2 * P
UB = B // P
NB = (TOP * TOKENS + E * (B - 1)) // B
NU = NB * UB
ROW = D + E
WST = HID + HC * D + HC + 1
RING = 6
AMONG = 1
LOOPED = (NB - 2) // RING * RING
HALF = TOKENS // 2
PACK1, PACK2 = {}, {}
for _pack, _parts in ((PACK1, (("bdA", P), ("bdAT", P), ("Istack", N), ("Bm", N), ("W_in", D), ("b_in", 1),
                               ("quadrant", G))),
                      (PACK2, (("bdC", J * D), ("gateT", GE), ("Dbc", D)))):
    _at = 0
    for _name, _n in _parts:
        _pack[_name] = slice(_at, _at + _n)
        _at += _n
    _pack["all"] = slice(0, _at)
CH = 8
BATCHES = TOP * COLS // CH
O1BUFS = 4
FIRST = slice(0, RING * UB)
REST = slice(RING * UB, NU)
ACT_BATCHES = (0,)
BEFORE_BLOCK = 4
FP16 = mybir.dt.float16
BF16 = mybir.dt.bfloat16
I32 = mybir.dt.int32


def build(nc, x, pack1, pack2, wall, xg, out):
    ctx = ExitStack()
    with ctx:
        def sb(name, shape, dt=FP32):
            return ctx.enter_context(nc.sbuf_tensor(name, shape, dt))

        def sem(name):
            return ctx.enter_context(nc.semaphore(name))

        bank = [ctx.enter_context(nc.psum_tensor(f"bank{k}", [P, 512], FP32)) for k in range(8)]

        x_sb = sb("x_sb", [P, TILES, J, D])
        p1 = sb("p1", [P, PACK1["all"].stop])
        p2 = sb("p2", [P, PACK2["all"].stop])
        w_sb = sb("w_sb", [P, E, WST])
        Bm_sb, Win_sb, bin_sb = (p1[0:N, PACK1[k]] for k in ("Bm", "W_in", "b_in"))
        Istack, gateT_sb, bdC = p1[:, PACK1["Istack"]], p2[:, PACK2["gateT"]], p2[:, PACK2["bdC"]]
        ident = sb("ident", [P, P])
        eiota = sb("eiota", [P, COLS, E])
        lower = sb("lower", [P, P], BF16)
        ones = sb("ones", [P, P], BF16)
        restart = sb("restart", [P, E, COLS])
        steps = sb("steps", [P, E, TOKENS // B])
        biota = sb("biota", [1, NB, E])
        riota = sb("riota", [P, P, CH], FP16)
        uiota = sb("uiota", [P, NU, CH], FP16)
        number = sb("number", [P, COLS], FP16)
        number32 = sb("number32", [P, COLS])
        spare = sb("spare", [P, NB, UB])
        zrow = sb("zrow", [P, ROW])
        pw = sb("pw", [P, J + 1, 2, P])
        sq = sb("sq", [P, DOUBLINGS, 2, P])
        BA = sb("BA", [N, 2 * J - 1, N])
        Gst = sb("Gst", [D, 2 * J - 1, N])
        hbias = sb("hbias", [P, 1])
        Cor = sb("Cor", [P, G, J * N])
        stats = sb("stats", [P, COLS, 6])
        mean = sb("mean", [P, COLS])
        var = sb("var", [P, COLS])
        sd = sb("sd", [P, COLS])
        rs = sb("rs", [P, COLS])
        nmr = sb("nmr", [P, COLS])
        tn = sb("tn", [P, COLS])
        warm = sb("warm", [P, 1])
        xd = sb("xd", [P, TILES, J, D])
        xh = sb("xh", [P, TILES, J, ROW])
        xhT = sb("xhT", [D, TILES, J, P])
        hfull = sb("hfull", [P, TILES, P])
        ebuf = sb("ebuf", [P, HALVES, SEQS, SEQ_CHUNKS + 1])
        gT = sb("gT", [P, HALVES, J * P])
        lg = sb("lg", [P, COLS, E])
        ex = sb("ex", [P, COLS, E])
        pr = sb("pr", [P, COLS, E])
        prob = sb("prob", [P, COLS, E])
        sums = sb("sums", [P, COLS, E // 2])
        inv = sb("inv", [P, 4, COLS])
        oh = sb("oh", [P, TOP, COLS, E])
        both = sb("both", [P, COLS, E], BF16)
        r1 = sb("r1", [P, 4, COLS])
        tot = sb("tot", [P, E, COLS])
        upto = sb("upto", [P, E, COLS])
        cmp_ = sb("cmp_", [P, E, TOKENS // B])
        nblk = sb("nblk", [P, E])
        cum = sb("cum", [P, E])
        first = sb("first", [P, E])
        bcmp = sb("bcmp", [1, NB, E])
        bexp = sb("bexp", [1, NB])
        bexp_i = sb("bexp_i", [1, NB], I32)
        slot = sb("slot", [P, TOP * COLS])
        slot_i = sb("slot_i", [P, 3, TOP * COLS], I32)
        place_unit = sb("place_unit", [P, 2, TOP * COLS], FP16)
        R = sb("R", [P, BATCHES, P, CH], FP16)
        O1 = sb("O1", [P, O1BUFS, NU, CH], FP16)
        O = sb("O", [P, BATCHES, NU, CH], FP16)
        dc = sb("dc", [P, 3, NU])
        idx = sb("idx", [P, NU], I32)
        xr = sb("xr", [P, RING, UB, ROW])
        xgT = sb("xgT", [D, 2, B])
        wst = sb("wst", [P, 2, WST])
        hsb = sb("hsb", [P, HC, B])
        yT = sb("yT", [D, B])
        ys = sb("ys", [P, 2, UB, D])

        s_pack1_in = sem("s_pack1_in")
        s_pack2_in = sem("s_pack2_in")
        s_x_in = [sem(f"s_x_in{k}") for k in range(HT)]
        s_weights_in = sem("s_weights_in")
        s_const = sem("s_const")
        s_ident_zero = sem("s_ident_zero")
        s_ident = sem("s_ident")
        s_zero_parts = sem("s_zero_parts")
        s_setup_product = sem("s_setup_product")
        s_setup_copied = sem("s_setup_copied")
        s_carry_product = sem("s_carry_product")
        s_carry_copied = sem("s_carry_copied")
        s_vector_step = sem("s_vector_step")
        s_gpsimd_step = sem("s_gpsimd_step")
        s_stats = sem("s_stats")
        s_variance = sem("s_variance")
        s_root = sem("s_root")
        s_inverse = sem("s_inverse")
        s_norm_vector = sem("s_norm_vector")
        s_norm_scalar = sem("s_norm_scalar")
        s_norm_gpsimd = sem("s_norm_gpsimd")
        s_norm_transposed = sem("s_norm_transposed")
        s_normT_copied = sem("s_normT_copied")
        s_own_states = sem("s_own_states")
        s_scan_state = [sem(f"s_scan_state{k}") for k in range(HALVES)]
        s_scan_product = [sem(f"s_scan_product{k}") for k in range(HALVES)]
        s_states = sem("s_states")
        s_states_copied = sem("s_states_copied")
        s_output = sem("s_output")
        s_xd = sem("s_xd")
        s_residual = sem("s_residual")
        s_gate_product = sem("s_gate_product")
        s_gate_copied = sem("s_gate_copied")
        s_logits = sem("s_logits")
        s_logits_shifted = sem("s_logits_shifted")
        s_exp = sem("s_exp")
        s_chosen = sem("s_chosen")
        s_share_sum = sem("s_share_sum")
        s_share_inverse = sem("s_share_inverse")
        s_shares = sem("s_shares")
        s_counts = sem("s_counts")
        s_place = sem("s_place")
        s_unit_first = sem("s_unit_first")
        s_number_first = sem("s_number_first")
        s_unit = sem("s_unit")
        s_number_vector = sem("s_number_vector")
        s_number_scalar = sem("s_number_scalar")
        s_numbers = sem("s_numbers")
        s_rows_known = sem("s_rows_known")
        s_experts_known = sem("s_experts_known")
        s_zero_row = sem("s_zero_row")
        s_residual_stored = sem("s_residual_stored")
        s_rows_stored = sem("s_rows_stored")
        s_gathered = [sem(f"s_gathered{k}") for k in range(RING)]
        s_rows_transposed = sem("s_rows_transposed")
        s_rowsT_copied = sem("s_rowsT_copied")
        s_weights_staged = sem("s_weights_staged")
        s_hidden_product = sem("s_hidden_product")
        s_hidden = sem("s_hidden")
        s_expert_product = sem("s_expert_product")
        s_expert_biased = sem("s_expert_biased")
        s_expert_transposed = sem("s_expert_transposed")
        s_scaled = sem("s_scaled")
        s_added = [sem(f"s_added{k}") for k in range(2)]

        block = ctx.enter_context(nc.Block())
        x_v = x.rearrange("(i q j) d -> q i (j d)", q=P, j=J)
        out_v = out[0:TOKENS, :].rearrange("(i q j) d -> i q (j d)", q=P, j=J)
        xg_v = xg[0:TOKENS, :].rearrange("(i q j) w -> i q j w", q=P, j=J)
        CONSTS = 3 + 10 + 2

        def norm_split(layer, i):
            if layer == 0:
                return (2 if i < HT else 3), J
            return (0, 3) if i < HT else (3, J)

        def normalised(engine, layer, i):
            engine.wait_ge(s_norm_scalar, TILES * layer + i + 1)
            if norm_split(layer, i)[0]:
                engine.wait_ge(s_norm_vector, (TILES - HT) * layer + i + 1)
            if norm_split(layer, i)[1] < J:
                engine.wait_ge(s_norm_gpsimd, i + 1)

        def made_before(engine, t):
            n = sum(a <= t for a in ACT_BATCHES)
            if t in ACT_BATCHES:
                engine.wait_ge(s_number_scalar, n)
            else:
                engine.wait_ge(s_number_vector, t + 1 - n)

        def scattered(k, turn=0):
            return 16 * UB * (turn * (RING // 2) + k // 2 + 2)

        @block.sync
        def _(sp):
            for h in range(HT):
                sp.dma_start(x_sb[:, 2 * h:2 * h + 2, :, :].rearrange("q i j d -> q i (j d)"),
                             x_v[:, 2 * h:2 * h + 2, :]).then_inc(s_x_in[h], 16)
            sp.dma_start(w_sb[:, :, :], wall).then_inc(s_weights_in, 16)
            with sp.Fori(0, TILES) as i:
                sp.wait_ge(s_residual, i + 1)
                sp.dma_start(out_v[bass.ds(i, 1)].rearrange("a q n -> q (a n)"),
                             x_sb[:, bass.ds(i, 1), :, :].rearrange("q a j d -> q (a j d)")
                             ).then_inc(s_residual_stored, 16)
            for i in range(TILES):
                normalised(sp, 1, i)
                sp.dma_start(xg_v[i, :, :, 0:D], xh[:, i, :, 0:D]).then_inc(s_rows_stored, 16)
            sp.wait_ge(s_shares, 1)
            for j in range(J):
                sp.dma_start(xg_v[:, :, j, D:ROW].rearrange("i q e -> q i e"),
                             xh[:, :, j, D:ROW]).then_inc(s_rows_stored, 16)

        @block.gpsimd
        def _(pool):
            nc.gpsimd.memset(ident[:], 0.0).then_inc(s_ident_zero, 1)
            pool.wait_ge(s_ident_zero, 1)
            nc.gpsimd.affine_select(out=ident[:], in_=ident[:], compare_op=ALU.not_equal, fill=1.0, base=0,
                                    pattern=[[-1, P]], channel_multiplier=1).then_inc(s_ident, 1)
            pool.wait_ge(s_pack2_in, 16)
            for i in range(TILES):
                pool.wait_ge(s_x_in[i // 2], 16)
                nc.gpsimd.tensor_tensor(xd[:, i, :, :], x_sb[:, i, :, :],
                                        p2[:, PACK2["Dbc"]].unsqueeze(1).to_broadcast([P, J, D]),
                                        ALU.add).then_inc(s_xd, 1)
            nc.gpsimd.memset(zrow[:], 0.0).then_inc(s_zero_row, 1)
            pool.wait_ge(s_zero_row, 1)
            for u in range(UB):
                past = TOKENS + P * u
                nc.gpsimd.dma_start(out[past:past + P, :], zrow[:, 0:D]).then_inc(s_added[0], 16)
                nc.gpsimd.dma_start(xg[past:past + P, :], zrow[:, :]).then_inc(s_added[1], 16)
            nc.gpsimd.memset(ones[:], 1.0).then_inc(s_const, 1)
            nc.gpsimd.memset(lower[:], 1.0).then_inc(s_const, 1)
            nc.gpsimd.memset(restart[:], 1.0).then_inc(s_const, 1)

            def count(dst, pattern, base=0, q=0):
                nc.gpsimd.iota(dst, pattern, base=base, channel_multiplier=q,
                               allow_small_or_imprecise_dtypes=True).then_inc(s_const, 1)

            count(eiota[:], [[0, COLS], [-1, E]], base=E)
            count(steps[:], [[0, E], [B, TOKENS // B]])
            count(biota[:], [[1, NB], [0, E]])
            count(riota[:], [[1, P], [0, CH]])
            count(uiota[:], [[1, NU], [0, CH]])
            for h in range(HALVES):
                for dst in (number, number32):
                    count(dst[:, h * HT * J:(h + 1) * HT * J], [[J * P, HT], [1, J]], base=(1 if h else -HALF), q=J)
            count(spare[:], [[0, NB], [P, UB]], base=TOKENS - HALF, q=1)
            pool.wait_ge(s_const, 3)
            nc.gpsimd.affine_select(out=lower[:], in_=lower[:], compare_op=ALU.is_gt, fill=0.0, base=0,
                                    pattern=[[1, P]], channel_multiplier=-1).then_inc(s_const, 1)
            nc.gpsimd.affine_select(out=restart[:], in_=restart[:], compare_op=ALU.not_equal, fill=0.0, base=0,
                                    pattern=[[0, E], [1, COLS]], channel_multiplier=0).then_inc(s_const, 1)

            pool.wait_ge(s_inverse, HALVES + 1)
            for i in range(HT):
                for j in range(norm_split(1, i)[1], J):
                    c = J * i + j
                    last = nc.gpsimd.tensor_scalar(xh[:, i, j, 0:D], x_sb[:, i, j, :], mean[:, c:c + 1],
                                                   rs[:, c:c + 1], ALU.subtract, ALU.mult)
                last.then_inc(s_norm_gpsimd, 1)

            pool.wait_ge(s_exp, HALVES)
            steps_done = [0]

            def done(ins):
                steps_done[0] += 1
                ins.then_inc(s_gpsimd_step, 1)
                pool.wait_ge(s_gpsimd_step, steps_done[0])

            def total(a):
                w = E // 2
                while w:
                    done(nc.gpsimd.tensor_tensor(sums[:, :, 0:w], a[:, :, 0:w], a[:, :, w:2 * w], ALU.add))
                    a, w = sums, w // 2

            def reciprocal(n):
                pool.wait_ge(s_share_inverse, n + 1)
                return inv[:, n, :].unsqueeze(2).to_broadcast([P, COLS, E])

            total(ex)
            nc.gpsimd.tensor_copy(inv[:, 2, :], sums[:, :, 0]).then_inc(s_share_sum, 1)
            done(nc.gpsimd.tensor_tensor(prob[:, :, :], ex[:, :, :], reciprocal(0), ALU.mult))
            pool.wait_ge(s_chosen, HALVES)
            done(nc.gpsimd.tensor_tensor(prob[:, :, :], prob[:, :, :], both[:, :, :], ALU.mult))
            total(prob)
            nc.gpsimd.tensor_copy(inv[:, 3, :], sums[:, :, 0]).then_inc(s_share_sum, 1)
            nc.gpsimd.tensor_tensor(xh[:, :, :, D:ROW].rearrange("q i j e -> q (i j) e"), prob[:, :, :],
                                    reciprocal(1), ALU.mult).then_inc(s_shares, 1)

            def gather(b):
                if b >= RING:
                    pool.wait_ge(s_scaled, b - RING + 1)
                for u in range(UB):
                    nc.gpsimd.indirect_dma_start(
                        out=xr[:, b % RING, u, :], out_offset=None, in_=xg,
                        in_offset=bass.IndirectOffsetOnAxis(ap=idx[:, UB * b + u:UB * b + u + 1], axis=0),
                    ).then_inc(s_gathered[b % RING], 16)

            def scatter(b):
                pool.wait_ge(s_scaled, b + 1)
                pool.wait_ge(s_added[(b + 1) % 2], scattered(b - 1))
                for u in range(UB):
                    nc.gpsimd.indirect_dma_start(
                        out=out, in_=ys[:, b % 2, u, :], in_offset=None, compute_op=ALU.add,
                        out_offset=bass.IndirectOffsetOnAxis(ap=idx[:, UB * b + u:UB * b + u + 1], axis=0),
                    ).then_inc(s_added[b % 2], 16)

            pool.wait_ge(s_rows_known, 1)
            pool.wait_ge(s_rows_stored, 16 * (TILES + J))
            pool.wait_ge(s_added[1], 16 * UB)
            for b in range(RING - 1):
                gather(b)
            pool.wait_ge(s_residual_stored, 16 * TILES)
            for b in range(NB):
                if b == 1:
                    pool.wait_ge(s_rows_known, 2)
                if b + RING - 1 < NB:
                    gather(b + RING - 1)
                scatter(b)
            for b in (NB - 2, NB - 1):
                pool.wait_ge(s_added[b % 2], scattered(b))

        @block.scalar
        def _(act):
            act.dma_start(p1[:, :], pack1).then_inc(s_pack1_in, 16)
            act.dma_start(p2[:, :], pack2).then_inc(s_pack2_in, 16)
            nc.scalar.activation(warm[:, :], nc.const_aps.tensor(1.0, (P, 1), FP32), ACT.Sqrt)

            def copy(dst, src, after):
                act.wait_ge(s_setup_product, after)
                return nc.scalar.activation(dst, src, ACT.Identity)

            def square(k):
                copy(sq[:, k, :, :], bank[6 + (k + 1) % 2][:, 0:2 * P], 5 + k).then_inc(s_setup_copied, 1)

            def root(n):
                c = slice(n % HALVES * HT * J, (n % HALVES + 1) * HT * J)
                act.wait_ge(s_variance, n + 1)
                nc.scalar.activation(sd[:, c], var[:, c], ACT.Sqrt).then_inc(s_root, 1)

            def normalise(layer, i):
                act.wait_ge(s_inverse, HALVES * layer + i // HT + 1)
                for j in range(*norm_split(layer, i)):
                    c = J * i + j
                    last = nc.scalar.activation(xh[:, i, j, 0:D], x_sb[:, i, j, :], ACT.Identity,
                                                bias=nmr[:, c:c + 1], scale=rs[:, c:c + 1])
                last.then_inc(s_norm_scalar, 1)

            def transposed(layer, i):
                act.wait_ge(s_norm_transposed, TILES * layer + i + 1)
                nc.scalar.activation(xhT[:, i, :, :], bank[i % 2][:, :], ACT.Identity).then_inc(s_normT_copied, 1)

            def gates(h):
                act.wait_ge(s_gate_product, HT * (h + 1))
                nc.scalar.activation(gT[:, h, :], bank[GATEBANK[h]][:, :], ACT.Identity).then_inc(s_gate_copied, 1)

            copy(pw[:, 2, :, :], bank[7][:, 0:2 * P], 1).then_inc(s_setup_copied, 1)
            copy(pw[:, 3:5, :, :], bank[6][:, :], 2).then_inc(s_setup_copied, 1)
            root(0)
            act.wait_ge(s_zero_parts, 1)
            copy(BA[:, J - 1:, :], bank[7][0:N, 0:P], 3).then_inc(s_setup_copied, 1)
            normalise(0, 0)
            copy(Gst[:, J - 1:, :], bank[6][:, 0:P], 4).then_inc(s_setup_copied, 1)
            normalise(0, 1)
            transposed(0, 0)
            normalise(0, 2)
            transposed(0, 1)
            normalise(0, 3)
            root(1)
            transposed(0, 2)
            transposed(0, 3)
            normalise(0, 4)
            normalise(0, 5)
            copy(hbias[:, :], bank[6][:, P:P + 1], 5).then_inc(s_setup_copied, 1)
            for i in range(4, TILES):
                transposed(0, i)
                if i + 2 < TILES:
                    normalise(0, i + 2)
                square(i - 3)
            square(5)
            for h in range(HALVES):
                act.wait_ge(s_states, h + 1)
                nc.scalar.activation(hfull[:, h * HT:(h + 1) * HT, :], bank[2 + h][:, :], ACT.Identity,
                                     bias=hbias[:, :]).then_inc(s_states_copied, 1)
            root(2)
            normalise(1, 0)
            for i in range(1, HT):
                normalise(1, i)
                transposed(1, i - 1)
            root(3)
            transposed(1, HT - 1)
            normalise(1, HT)
            gates(0)
            for i in range(HT + 1, TILES):
                normalise(1, i)
                transposed(1, i - 1)
            transposed(1, TILES - 1)
            gates(1)
            for h in range(HALVES):
                act.wait_ge(s_logits_shifted, h + 1)
                c = slice(h * HT * J, (h + 1) * HT * J)
                nc.scalar.activation(ex[:, c, :], lg[:, c, :], ACT.Exp).then_inc(s_exp, 1)

            def stage(b, k):
                e = nc.scalar.value_load(bexp_i[0:1, bass.ds(b, 1)], min_val=0, max_val=E - 1)
                nc.scalar.activation(wst[:, k % 2, :], w_sb[:, bass.ds(e, 1), :].rearrange("p a n -> p (a n)"),
                                     ACT.Identity).then_inc(s_weights_staged, 1)

            def hidden(b, k):
                for c in range(HC):
                    act.wait_ge(s_hidden_product, HC * b + c + 1)
                    nc.scalar.activation(hsb[:, c, :], bank[c][:, 0:B], ACT.Relu,
                                         bias=wst[:, k % 2, WST - 1 - HC + c:WST - HC + c]).then_inc(s_hidden, 1)

            act.wait_ge(s_const, CONSTS)
            for t in ACT_BATCHES:
                act.wait_ge(s_unit, t + 1)
                for c in range(CH):
                    n = (t * CH + c) % COLS
                    last = nc.scalar.activation(O[:, t, REST, c], O1[:, t % O1BUFS, REST, c], ACT.Copy,
                                                scale=number32[:, n:n + 1])
                last.then_inc(s_number_scalar, 1)
            act.wait_ge(s_weights_in, 16)
            act.wait_ge(s_experts_known, 1)
            stage(0, 0)
            stage(1, 1)
            act.wait_ge(s_weights_staged, 2)
            hidden(0, 0)
            with act.Fori(0, LOOPED // RING) as turn:
                for k in range(RING):
                    b = RING * turn + k
                    hidden(b + 1, k + 1)
                    act.wait_ge(s_expert_biased, b + 1)
                    stage(b + 2, k)
                    act.wait_ge(s_weights_staged, b + 3)
            for b in range(LOOPED, NB):
                if b + 1 < NB:
                    hidden(b + 1, b + 1)
                if b + 2 < NB:
                    act.wait_ge(s_expert_biased, b + 1)
                    stage(b + 2, b)
                    act.wait_ge(s_weights_staged, b + 3)

        @block.vector
        def _(dve):
            chain = [0]

            def link(ins):
                chain[0] += 1
                ins.then_inc(s_vector_step, 1)
                dve.wait_ge(s_vector_step, chain[0])

            def wide(a, n=E):
                return a.unsqueeze(2).to_broadcast([P, a.shape[1], n])

            nc.vector.memset(BA[:, 0:J - 1, :], 0.0)
            nc.vector.memset(Gst[:, 0:J - 1, :], 0.0).then_inc(s_zero_parts, 1)
            link(nc.vector.memset(ebuf[:], 0.0))

            def statistics(i):
                for j in range(J):
                    last = nc.vector.bn_stats(stats[:, J * i + j, :], x_sb[:, i, j, :])
                last.then_inc(s_stats, 1)

            def variance(n):
                c = slice(n % HALVES * HT * J, (n % HALVES + 1) * HT * J)
                even, odd = stats[:, c, 0:3], stats[:, c, 3:6]
                dve.wait_ge(s_stats, HT * (n + 1))
                nc.vector.tensor_tensor(mean[:, c], even[:, :, 1], odd[:, :, 1], ALU.add)
                nc.vector.tensor_tensor(tn[:, c], even[:, :, 1], odd[:, :, 1], ALU.subtract)
                link(nc.vector.scalar_tensor_tensor(var[:, c], even[:, :, 2], D * EPS, odd[:, :, 2],
                                                    ALU.add, ALU.add))
                nc.vector.tensor_scalar(mean[:, c], mean[:, c], 0.5, None, ALU.mult)
                link(nc.vector.scalar_tensor_tensor(tn[:, c], tn[:, c], 0.25, tn[:, c], ALU.mult, ALU.mult))
                nc.vector.scalar_tensor_tensor(var[:, c], var[:, c], 1.0 / D, tn[:, c],
                                               ALU.mult, ALU.add).then_inc(s_variance, 1)

            def inverse(n):
                c = slice(n % HALVES * HT * J, (n % HALVES + 1) * HT * J)
                dve.wait_ge(s_root, n + 1)
                link(nc.vector.reciprocal(rs[:, c], sd[:, c]))
                link(nc.vector.tensor_tensor(tn[:, c], rs[:, c], rs[:, c], ALU.mult))
                link(nc.vector.scalar_tensor_tensor(tn[:, c], tn[:, c], -0.5, var[:, c], ALU.mult, ALU.mult))
                link(nc.vector.scalar_tensor_tensor(rs[:, c], tn[:, c], 1.5, rs[:, c], ALU.add, ALU.mult))
                nc.vector.scalar_tensor_tensor(nmr[:, c], mean[:, c], -1.0, rs[:, c],
                                               ALU.mult, ALU.mult).then_inc(s_inverse, 1)

            def normalise(layer, i):
                for j in range(norm_split(layer, i)[0]):
                    c = J * i + j
                    last = nc.vector.tensor_scalar(xh[:, i, j, 0:D], x_sb[:, i, j, :], mean[:, c:c + 1],
                                                   rs[:, c:c + 1], ALU.subtract, ALU.mult)
                last.then_inc(s_norm_vector, 1)

            for i in range(HT):
                dve.wait_ge(s_x_in[i // 2], 16)
                statistics(i)
            variance(0)
            dve.wait_ge(s_x_in[HT // 2], 16)
            statistics(HT)
            inverse(0)
            for i in range(HT):
                normalise(0, i)
            for i in range(HT + 1, TILES):
                dve.wait_ge(s_x_in[i // 2], 16)
                statistics(i)
            variance(1)
            inverse(1)
            for i in range(HT, TILES):
                normalise(0, i)

            def ends(h):
                dve.wait_ge(s_own_states, h + 1)
                dve.wait_ge(s_setup_copied, 5)
                for g in range(G):
                    last = nc.vector.tensor_scalar(
                        ebuf[N * g:N * g + N, h, :, 1:],
                        bank[2 + h][P - N:P, g * P:g * P + P].rearrange("n (s c) -> n s c", c=SEQ_CHUNKS),
                        hbias[P - N:P, :], None, ALU.add)
                last.then_inc(s_scan_state[h], 1)

            def doubled(h, k):
                step = 1 << k
                dve.wait_ge(s_scan_state[h], k + 1)
                dve.wait_ge(s_scan_product[h], k + 1)
                nc.vector.tensor_tensor(
                    ebuf[:, h, :, 1 + step:], ebuf[:, h, :, 1 + step:],
                    bank[SCANBANK[h]][:, 0:P].rearrange("n (s c) -> n s c", c=SEQ_CHUNKS)[:, :, 0:SEQ_CHUNKS - step],
                    ALU.add).then_inc(s_scan_state[h], 1)

            ends(0)
            for k in range(3):
                doubled(0, k)
            ends(1)
            for k in range(2):
                doubled(0, k + 3)
                doubled(1, k)
            dve.wait_ge(s_carry_product, 1)
            nc.vector.tensor_tensor(
                Cor[:, :, :], bank[CARRYBANK][:, 0:P].unsqueeze(1).to_broadcast([P, G, J * N]),
                wide(p1[:, PACK1["quadrant"]], J * N), ALU.mult).then_inc(s_carry_copied, 1)
            doubled(0, 5)
            doubled(1, 2)

            def residual(i):
                dve.wait_ge(s_xd, i + 1)
                dve.wait_ge(s_output, i + 1)
                nc.vector.tensor_tensor(x_sb[:, i, :, :], xd[:, i, :, :],
                                        bank[YBANKS[i % len(YBANKS)]][:, :].rearrange("q (j d) -> q j d", j=J),
                                        ALU.add).then_inc(s_residual, 1)

            def after_residual(i):
                dve.wait_ge(s_residual, i + 1)
                statistics(i)

            doubled(1, 3)
            residual(0)
            doubled(1, 4)
            after_residual(0)
            residual(1)
            doubled(1, 5)
            after_residual(1)
            for i in (2, 3):
                residual(i)
                after_residual(i)
            variance(2)
            residual(HT)
            inverse(2)
            after_residual(HT)
            for i in range(HT + 1, TILES):
                residual(i)
                after_residual(i)
            variance(3)
            inverse(3)
            dve.wait_ge(s_inverse, 4)
            for i in range(HT, TILES):
                normalise(1, i)

            dve.wait_ge(s_const, CONSTS)
            for h in range(HALVES):
                c = slice(h * HT * J, (h + 1) * HT * J)
                G4 = bank[2 + h][:, :].rearrange("p (j g w) -> p g j w", g=HT, w=GE)[:, :, :, 0:E]
                top4 = r1[:, 0, c].rearrange("p (g j) -> p g j", j=J)
                dve.wait_ge(s_logits, h + 1)
                link(nc.vector.tensor_reduce(top4, G4, AX.X, ALU.max))
                nc.vector.tensor_tensor(lg[:, c, :].rearrange("p (g j) e -> p g j e", j=J), G4,
                                        top4.unsqueeze(3).to_broadcast([P, HT, J, E]),
                                        ALU.subtract).then_inc(s_logits_shifted, 1)
                dve.wait_ge(s_logits_shifted, h + 1)
                link(nc.vector.scalar_tensor_tensor(pr[:, c, :], lg[:, c, :], 0.0, eiota[:, c, :],
                                                    ALU.is_equal, ALU.mult))
                link(nc.vector.tensor_reduce(r1[:, 1, c], pr[:, c, :], AX.X, ALU.max))
                link(nc.vector.tensor_tensor(oh[:, 0, c, :], eiota[:, c, :], wide(r1[:, 1, c]), ALU.is_equal))
                link(nc.vector.scalar_tensor_tensor(pr[:, c, :], oh[:, 0, c, :], -3e38, lg[:, c, :],
                                                    ALU.mult, ALU.add))
                link(nc.vector.tensor_reduce(r1[:, 2, c], pr[:, c, :], AX.X, ALU.max))
                link(nc.vector.tensor_tensor(pr[:, c, :], pr[:, c, :], wide(r1[:, 2, c]), ALU.is_equal))
                link(nc.vector.tensor_tensor(pr[:, c, :], pr[:, c, :], eiota[:, c, :], ALU.mult))
                link(nc.vector.tensor_reduce(r1[:, 3, c], pr[:, c, :], AX.X, ALU.max))
                link(nc.vector.tensor_tensor(oh[:, 1, c, :], eiota[:, c, :], wide(r1[:, 3, c]), ALU.is_equal))
                nc.vector.tensor_tensor(both[:, c, :], oh[:, 0, c, :], oh[:, 1, c, :], ALU.add).then_inc(s_chosen, 1)
            def invert(n):
                dve.wait_ge(s_share_sum, n + 1)
                nc.vector.reciprocal(inv[:, n, :], inv[:, 2 + n, :]).then_inc(s_share_inverse, 1)

            invert(0)
            dve.wait_ge(s_counts, 1)
            counts = bank[1][:, 0:E * COLS]
            link(nc.vector.tensor_tensor_scan(upto[:, :, :].rearrange("p e t -> p (e t)"),
                                              restart[:, :, :].rearrange("p e t -> p (e t)"),
                                              counts, 0.0, ALU.mult, ALU.add))
            nc.vector.tensor_tensor(tot[:, :, :].rearrange("p e t -> p (e t)"),
                                    upto[:, :, :].rearrange("p e t -> p (e t)"), counts, ALU.subtract)
            link(nc.vector.tensor_tensor(cmp_[:, :, :], wide(upto[:, :, COLS - 1], TOKENS // B), steps[:, :, :],
                                         ALU.is_gt))
            link(nc.vector.tensor_reduce(nblk[:, :], cmp_[:, :, :], AX.X, ALU.add))
            link(nc.vector.tensor_tensor_scan(cum[:, :], ones[:, 0:E], nblk[:, :], 0.0, ALU.mult, ALU.add))
            link(nc.vector.tensor_tensor(first[:, :], cum[:, :], nblk[:, :], ALU.subtract))
            link(nc.vector.scalar_tensor_tensor(tot[:, :, :], wide(first[:, :], COLS), float(B), tot[:, :, :],
                                                ALU.mult, ALU.add))
            link(nc.vector.tensor_tensor(lg[:, :, :], bank[0][:, 0:COLS * E].rearrange("p (t e) -> p t e", e=E),
                                         tot[:, :, :].rearrange("p e t -> p t e"), ALU.add))
            pairs = oh[:, :, :, :].rearrange("p k t e -> p k (t e)")
            link(nc.vector.tensor_tensor(pairs, pairs, lg[:, :, :].rearrange("p t e -> p (t e)").unsqueeze(1)
                                         .to_broadcast([P, TOP, COLS * E]), ALU.mult))
            link(nc.vector.tensor_reduce(slot[:, :], oh[:, :, :, :].rearrange("p k t e -> p (k t) e"), AX.X, ALU.add))
            link(nc.vector.tensor_copy(slot_i[:, 0, :], slot[:, :]))
            nc.vector.tensor_scalar(slot_i[:, 1, :], slot_i[:, 0, :], P - 1, None, ALU.bitwise_and)
            link(nc.vector.tensor_scalar(slot_i[:, 2, :], slot_i[:, 0, :], P.bit_length() - 1, None,
                                         ALU.logical_shift_right))
            link(nc.vector.tensor_copy(place_unit[:, :, :], slot_i[:, 1:3, :]))

            def unit(t, units, signal):
                u = range(NU)[units]
                nc.vector.tensor_tensor(O1[:, t % O1BUFS, units, :], uiota[:, units, :],
                                        place_unit[:, 1, t * CH:t * CH + CH].unsqueeze(1).to_broadcast(
                                            [P, len(u), CH]), ALU.is_equal).then_inc(signal, 1)

            def number_of(t, units, signal):
                u = range(NU)[units]
                m = slice(t * CH % COLS, t * CH % COLS + CH)
                nc.vector.tensor_tensor(O[:, t, units, :], O1[:, t % O1BUFS, units, :],
                                        number[:, m].unsqueeze(1).to_broadcast([P, len(u), CH]),
                                        ALU.mult).then_inc(signal, 1)

            for t in range(BATCHES):
                if t >= O1BUFS:
                    dve.wait_ge(s_number_first, t - O1BUFS + 1)
                unit(t, FIRST, s_unit_first)
                nc.vector.tensor_tensor(R[:, t, :, :], riota[:, :, :],
                                        place_unit[:, 0, t * CH:t * CH + CH].unsqueeze(1).to_broadcast([P, P, CH]),
                                        ALU.is_equal).then_inc(s_place, 1)
                dve.wait_ge(s_unit_first, t + 1)
                number_of(t, FIRST, s_number_first)
                if t == 0:
                    invert(1)

            def decode(units, table, n):
                dve.wait_ge(s_numbers, n)
                link(nc.vector.tensor_copy(dc[:, 0, units], table))
                nc.vector.scalar_tensor_tensor(dc[:, 1, units], dc[:, 0, units], 0.0,
                                               spare[:, :, :].rearrange("p b u -> p (b u)")[:, units],
                                               ALU.is_equal, ALU.mult)
                link(nc.vector.scalar_tensor_tensor(dc[:, 2, units], dc[:, 0, units], 0.0, dc[:, 0, units],
                                                    ALU.is_gt, ALU.subtract))
                nc.vector.scalar_tensor_tensor(idx[:, units], dc[:, 1, units], float(HALF), dc[:, 2, units],
                                               ALU.add, ALU.subtract).then_inc(s_rows_known, 1)

            unit(0, REST, s_unit)
            decode(FIRST, bank[4][:, FIRST], 1)

            link(nc.vector.tensor_tensor(bcmp[:, :, :], biota[:, :, :],
                                         cum[0:1, :].unsqueeze(1).to_broadcast([1, NB, E]), ALU.is_ge))
            link(nc.vector.tensor_reduce(bexp[:, :], bcmp[:, :, :], AX.X, ALU.add))
            nc.vector.tensor_scalar(bexp_i[:, :], bexp[:, :], float(E - 1), None,
                                    ALU.min).then_inc(s_experts_known, 1)

            def rows_in(b, k):
                dve.wait_ge(s_rows_transposed, b + 1)
                nc.vector.tensor_copy(xgT[:, k % 2, :], bank[6][:, 0:B]).then_inc(s_rowsT_copied, 1)

            def rows_out(turn, k):
                b = RING * turn + k
                dve.wait_ge(s_expert_product, b + 1)
                nc.vector.tensor_scalar(yT[:, :], bank[4][:, 0:B], wst[:, k % 2, WST - 1:WST], None,
                                        ALU.add).then_inc(s_expert_biased, 1)
                e = nc.vector.value_load(bexp_i[0:1, bass.ds(b, 1)], min_val=0, max_val=E - 1)
                dve.wait_ge(s_expert_transposed, b + 1)
                dve.wait_ge(s_added[k % 2], scattered(k - 2, turn))
                for u in range(UB):
                    last = nc.vector.tensor_scalar(ys[:, k % 2, u, :], bank[5][:, u * P:u * P + P],
                                                   xr[:, k, u, bass.ds(e + D, 1)], None, ALU.mult)
                last.then_inc(s_scaled, 1)

            for t in range(BATCHES):
                if t + 1 < BATCHES:
                    if t + 1 >= O1BUFS:
                        made_before(dve, t + 1 - O1BUFS)
                    unit(t + 1, REST, s_unit)
                if t not in ACT_BATCHES:
                    dve.wait_ge(s_unit, t + 1)
                    number_of(t, REST, s_number_vector)
                if t == BEFORE_BLOCK:
                    rows_in(0, 0)
            decode(REST, bank[7][:, REST], 2)
            dve.wait_ge(s_weights_staged, 2)
            rows_in(1, 1)
            with dve.Fori(0, LOOPED // RING) as turn:
                for k in range(RING):
                    b = RING * turn + k
                    rows_out(turn, k)
                    rows_in(b + 2, k)
            for b in range(LOOPED, NB):
                turn, k = b // RING, b % RING
                rows_out(turn, k)
                if b + 2 < NB:
                    rows_in(b + 2, k)

        @block.tensor
        def _(pe):
            mm = nc.tensor.matmul

            def product(dst, lhsT, rhs, start=True, stop=True):
                return mm(dst, lhsT, rhs, start=start, stop=stop)

            bdA, bdAT = p1[:, PACK1["bdA"]], p1[:, PACK1["bdAT"]]
            pe.wait_ge(s_pack1_in, 16)
            product(bank[7][:, 0:P], bdAT, bdA)
            product(bank[7][:, P:2 * P], bdA, bdAT).then_inc(s_setup_product, 1)
            pe.wait_ge(s_setup_copied, 1)
            product(bank[6][:, 0:P], bdAT, pw[:, 2, 0, :])
            product(bank[6][:, P:2 * P], bdA, pw[:, 2, 1, :])
            product(bank[6][:, 2 * P:3 * P], pw[:, 2, 1, :], pw[:, 2, 0, :])
            product(bank[6][:, 3 * P:4 * P], pw[:, 2, 0, :], pw[:, 2, 1, :]).then_inc(s_setup_product, 1)
            pe.wait_ge(s_setup_copied, 2)
            pe.wait_ge(s_ident, 1)
            for k, power in enumerate((ident[0:N, 0:N], p1[0:N, 0:N], pw[0:N, 2, 0, 0:N], pw[0:N, 3, 0, 0:N])):
                last = product(bank[7][0:N, k * N:k * N + N], Bm_sb, power)
            last.then_inc(s_setup_product, 1)
            pe.wait_ge(s_setup_copied, 3)
            product(bank[6][:, 0:P], Win_sb,
                    BA[:, J - 1:, :].rearrange("n k m -> n (k m)")).then_inc(s_setup_product, 1)

            def bias():
                for i in range(J):
                    last = product(bank[6][:, P:P + 1],
                                   BA[:, J - 1 - i:2 * J - 1 - i, :].rearrange("n k m -> n (k m)"),
                                   bin_sb, start=(i == 0), stop=(i == J - 1))
                last.then_inc(s_setup_product, 1)

            def carry():
                for j, powerT in enumerate((bdAT, pw[:, 2, 1, :], pw[:, 3, 1, :], pw[:, 4, 1, :])):
                    last = product(bank[CARRYBANK][:, j * N:j * N + N], powerT, Istack)
                last.then_inc(s_carry_product, 1)

            def square(k):
                pe.wait_ge(s_setup_copied, 4 + k)
                m, mT = (pw[:, 4, 0, :], pw[:, 4, 1, :]) if k == 1 else (sq[:, k - 1, 0, :], sq[:, k - 1, 1, :])
                product(bank[6 + (k + 1) % 2][:, 0:P], mT, m)
                product(bank[6 + (k + 1) % 2][:, P:2 * P], m, mT).then_inc(s_setup_product, 1)

            def transposes(layer, i):
                normalised(pe, layer, i)
                for j in range(J):
                    last = nc.tensor.transpose(bank[i % 2][:, j * P:j * P + P], xh[:, i, j, 0:D], ident[:, :])
                last.then_inc(s_norm_transposed, 1)

            def own(i):
                pe.wait_ge(s_normT_copied, i + 1)
                for j in range(J):
                    last = mm(bank[2 + i // HT][:, i % HT * P:i % HT * P + P],
                              Gst[:, J - 1 - j:2 * J - 1 - j, :].rearrange("d k n -> d (k n)"), xhT[:, i, j, :],
                              start=(i % HT == 0 and j == 0), stop=(j == J - 1), skip_group_check=True)
                if i % HT == HT - 1:
                    last.then_inc(s_own_states, 1)

            def double(h, k):
                pe.wait_ge(s_scan_state[h], k + 1)
                if k:
                    pe.wait_ge(s_setup_copied, 5 + k)
                mm(bank[SCANBANK[h]][:, 0:P].rearrange("n (s c) -> n s c", c=SEQ_CHUNKS),
                   sq[:, k, 0, :] if k else pw[:, 4, 0, :], ebuf[:, h, :, 1:],
                   start=True, stop=True).then_inc(s_scan_product[h], 1)

            def states(h):
                pe.wait_ge(s_scan_state[h], DOUBLINGS + 1)
                pe.wait_ge(s_carry_copied, 1)
                for g in range(G):
                    last = mm(bank[2 + h][:, g * P:g * P + P].rearrange("n (s c) -> n s c", c=SEQ_CHUNKS),
                              Cor[:, g, :], ebuf[:, h, :, 0:SEQ_CHUNKS],
                              start=False, stop=True, skip_group_check=True)
                last.then_inc(s_states, 1)

            transposes(0, 0)
            transposes(0, 1)
            pe.wait_ge(s_setup_copied, 4)
            own(0)
            transposes(0, 2)
            own(1)
            transposes(0, 3)
            own(2)
            bias()
            transposes(0, 4)
            own(3)
            square(1)
            for i in range(5, TILES):
                transposes(0, i)
                own(i - 1)
                square(i - 3)
                if i > 5:
                    double(0, i - 6)
            own(TILES - 1)
            double(0, 2)
            square(5)
            carry()

            def output(i):
                if i >= len(YBANKS):
                    pe.wait_ge(s_residual, i - len(YBANKS) + 1)
                mm(bank[YBANKS[i % len(YBANKS)]][:, :], hfull[:, i, :], bdC,
                   start=True, stop=True).then_inc(s_output, 1)

            def gate(i):
                pe.wait_ge(s_normT_copied, TILES + i + 1)
                g = i % HT
                mm(bank[GATEBANK[i // HT]][GE * g:GE * g + GE, :], gateT_sb, xhT[:, i, :, :],
                   start=True, stop=True).then_inc(s_gate_product, 1)

            def logits(h):
                pe.wait_ge(s_gate_copied, h + 1)
                for j in range(J):
                    m = slice(j * P, j * P + P)
                    last = nc.tensor.transpose(bank[2 + h][:, m], gT[:, h, m], ident[:, :])
                last.then_inc(s_logits, 1)

            pe.wait_ge(s_pack2_in, 16)
            double(0, 3)
            double(1, 0)
            double(0, 4)
            double(1, 1)
            double(0, 5)
            double(1, 2)
            states(0)
            double(1, 3)
            pe.wait_ge(s_states_copied, 1)
            output(0)
            double(1, 4)
            output(1)
            double(1, 5)
            output(2)
            states(1)
            output(3)
            pe.wait_ge(s_states_copied, 2)
            for i in range(HT, TILES):
                output(i)
            for i in range(HT):
                transposes(1, i)
            for i in range(HT):
                gate(i)
            transposes(1, HT)
            logits(0)
            for i in range(HT + 1, TILES):
                transposes(1, i)
            for i in range(HT, TILES):
                gate(i)
            logits(1)

            pe.wait_ge(s_const, CONSTS)
            pe.wait_ge(s_chosen, HALVES)
            mm(bank[0][:, 0:COLS * E], lower[:, :], both[:, :, :].rearrange("p t e -> p (t e)"),
               start=True, stop=True)
            mm(bank[1][:, 0:E * COLS].rearrange("p (e t) -> p e t", t=COLS), ones[:, :],
               both[:, :, :].rearrange("p t e -> p e t"),
               start=True, stop=True).then_inc(s_counts, 1)
            def slots(t, units, table):
                for c in range(CH):
                    last = mm(table, R[:, t, :, c], O[:, t, units, c],
                              start=(t == 0 and c == 0), stop=(t == BATCHES - 1 and c == CH - 1))
                if t == BATCHES - 1:
                    last.then_inc(s_numbers, 1)

            for t in range(BATCHES):
                pe.wait_ge(s_place, t + 1)
                pe.wait_ge(s_number_first, t + 1)
                slots(t, FIRST, bank[4][:, FIRST])

            def rows_in(turn, k):
                pe.wait_ge(s_gathered[k], 16 * UB * (turn + 1))
                for u in range(UB):
                    last = nc.tensor.transpose(bank[6][:, u * P:u * P + P], xr[:, k, u, 0:D], ident[:, :])
                last.then_inc(s_rows_transposed, 1)

            def up(b, k, out_of=None):
                pe.wait_ge(s_weights_staged, b + 1)
                pe.wait_ge(s_rowsT_copied, b + 1)
                for c in range(HC):
                    mm(bank[c][:, 0:B], wst[:, k % 2, c * P:c * P + P], xgT[:, k % 2, :],
                       start=True, stop=True).then_inc(s_hidden_product, 1)
                    if c == AMONG and out_of is not None:
                        rows_out(out_of)

            def down(b, k):
                for c in range(HC):
                    pe.wait_ge(s_hidden, HC * b + c + 1)
                    last = mm(bank[4][:, 0:B], wst[:, k % 2, HID + c * D:HID + c * D + D], hsb[:, c, :],
                              start=(c == 0), stop=(c == HC - 1))
                last.then_inc(s_expert_product, 1)

            def rows_out(b):
                pe.wait_ge(s_expert_biased, b + 1)
                for u in range(UB):
                    last = nc.tensor.transpose(bank[5][:, u * P:u * P + P], yT[:, u * P:u * P + P], ident[:, :])
                last.then_inc(s_expert_transposed, 1)

            for t in range(BATCHES):
                made_before(pe, t)
                slots(t, REST, bank[7][:, REST])
                if t == BEFORE_BLOCK - 1:
                    rows_in(0, 0)
                if t == BEFORE_BLOCK:
                    up(0, 0)
            rows_in(0, 1)
            down(0, 0)
            with pe.Fori(0, LOOPED // RING) as turn:
                for k in range(RING):
                    b = RING * turn + k
                    up(b + 1, k + 1, b)
                    rows_in(turn + (k + 2) // RING, (k + 2) % RING)
                    down(b + 1, k + 1)
            for b in range(LOOPED, NB):
                if b + 1 < NB:
                    up(b + 1, b + 1, b)
                else:
                    rows_out(b)
                if b + 2 < NB:
                    rows_in((b + 2) // RING, (b + 2) % RING)
                if b + 1 < NB:
                    down(b + 1, b + 1)


def kernel(L0_attn_x, L0_attn_A, L0_attn_Bm, L0_attn_C, L0_attn_D, L0_attn_W_in, L0_attn_b_in,
           L0_ffn_gate_w, L0_ffn_w1, L0_ffn_b1, L0_ffn_w2, L0_ffn_b2):
    import numpy as np
    import concourse.bacc as bacc
    from concourse.bass_utils import run_bass_kernel_spmd

    a = [np.asarray(v) for v in (L0_attn_x, L0_attn_A, L0_attn_Bm, L0_attn_C, L0_attn_D, L0_attn_W_in, L0_attn_b_in,
                                 L0_ffn_gate_w, L0_ffn_w1, L0_ffn_b1, L0_ffn_w2, L0_ffn_b2)]
    x, A, Bm, C, Dv, W_in, b_in, gate_w, w1, b1, w2, b2 = a

    def spread(block, rows, step):
        a = np.zeros((G * rows, G * step), block.dtype)
        for g in range(G):
            a[g * rows:(g + 1) * rows, g * step:g * step + block.shape[1]] = block
        return a

    def top(a):
        return np.concatenate([a, np.zeros((P - N, a.shape[1]), a.dtype)])

    laid = {
        "x": x.reshape(TILES * J * P, D),
        "pack1": np.concatenate([spread(A, N, N), spread(A.T, N, N), np.tile(np.eye(N, dtype=A.dtype), (G, 1)),
                                 top(Bm), top(W_in), top(b_in.reshape(N, 1)),
                                 np.kron(np.eye(G, dtype=A.dtype), np.ones((N, 1), A.dtype))], axis=1),
        "pack2": np.concatenate([spread(C.T, N, D), gate_w.T, np.zeros((D, GE - E), gate_w.dtype),
                                 np.tile(Dv, (P, 1))], axis=1),
        "wall": np.concatenate([w1.transpose(2, 0, 1),
                                w2.transpose(0, 2, 1).reshape(E, HC, P, D).transpose(2, 0, 1, 3).reshape(
                                    P, E, HC * D),
                                b1.reshape(E, HC, P).transpose(2, 0, 1), b2.T.reshape(D, E, 1)], axis=2),
    }
    laid = {k: np.ascontiguousarray(v) for k, v in laid.items()}
    nc = bacc.Bacc("TRN2", target_bir_lowering=False, num_devices=1)
    args = [nc.dram_tensor(k, v.shape, mybir.dt.float32, kind="ExternalInput").ap() for k, v in laid.items()]
    by = dict(zip(laid, args))
    out = nc.dram_tensor("out", (TOKENS + B, D), mybir.dt.float32, kind="ExternalOutput").ap()
    xg = nc.dram_tensor("xg", (TOKENS + B, ROW), mybir.dt.float32, kind="Internal").ap()
    build(nc, by["x"], by["pack1"], by["pack2"], by["wall"], xg, out)
    r = run_bass_kernel_spmd(nc, [laid], core_ids=[0])
    return r.results[0]["out"][0:TOKENS].reshape(x.shape)
```
